# Optimizing a Trainium2 kernel written in Bass

```python
import numpy as np
import jax
import jax.numpy as jnp

def _softmax(x, axis=-1):
    return jax.nn.softmax(x, axis=axis)

def _gelu(x):
    return jax.nn.gelu(x, approximate=True)

def _silu(x):
    return jax.nn.silu(x)

def _sigmoid(x):
    return jax.nn.sigmoid(x)

def _layernorm(x, axis=-1, eps=1e-05):
    m = jnp.mean(x, axis=axis, keepdims=True)
    v = jnp.var(x, axis=axis, keepdims=True)
    return (x - m) / jnp.sqrt(v + eps)

def _scatter_add(tgt, idx, src, axis=0):
    return tgt.at[idx].add(src)

def _segment_sum(src, seg, n):
    return jax.ops.segment_sum(src, seg, n)
kernel_name = 'mk_adj_resnorm_d2_adj_r2_7b6e1e'

def setup_inputs(seed: int=0):
    np.random.seed(seed)
    _w = jnp.asarray

    def _rec_inputs():
        import jax
        import jax.numpy as jnp
        _gk = jax.random.key(seed)
        x = 0.5 + 0.2887 * jax.random.normal(jax.random.fold_in(_gk, 1), (2048, 512), jnp.float32)
        _a = jax.random.bernoulli(jax.random.fold_in(_gk, 2), 0.00390625, (2048, 2048))
        _a = jnp.logical_or(_a, jnp.swapaxes(_a, -1, -2))
        _a = jnp.logical_or(_a, jnp.eye(2048, dtype=bool))
        _af = _a.astype(jnp.float32)
        _af = _af * jax.random.uniform(jax.random.fold_in(_gk, 3), (2048, 2048), jnp.float32, 0.05, 1)
        adj = _af
        return (x, adj)
    x, adj = _rec_inputs()

    def _L0_gnn_setup():
        import jax, jax.numpy as jnp
        import numpy as np
        NBITS = 4
        N_NODES = 4096
        IN_F = 512
        OUT_F = 512

        def _act_quant(x, alpha, b):
            n = float(2 ** b - 1)
            xd = x / alpha
            xc = jnp.minimum(xd, 1.0)
            xq = jnp.round(xc * n) / n
            return xq * alpha

        def _weight_quant(w, alpha, b):
            n = float(2 ** b - 1)
            wd = w / alpha
            wc = jnp.clip(wd, -1.0, 1.0)
            wq = jnp.round(jnp.abs(wc) * n) / n * jnp.sign(wc)
            return wq * alpha
        key = jax.random.key(seed)
        k1, k2, k3 = jax.random.split(key, 3)
        stdv = 1.0 / np.sqrt(OUT_F)
        inp = {'input': jax.random.uniform(k1, (N_NODES, IN_F), dtype=jnp.float32), 'adj': jax.random.uniform(k2, (N_NODES, N_NODES), dtype=jnp.float32), 'adj_scaling_factor': jnp.float32(2.0), 'weight': jax.random.uniform(k3, (IN_F, OUT_F), minval=-stdv, maxval=stdv, dtype=jnp.float32), 'wgt_alpha': jnp.float32(3.0), 'act_alpha': jnp.float32(1.0), 'act_alpha2': jnp.float32(1.0)}
        return inp
    _L0_gnn_all = _L0_gnn_setup()
    _L0_gnn_in = {k: v for k, v in _L0_gnn_all.items() if k in ('adj_scaling_factor', 'weight', 'wgt_alpha', 'act_alpha', 'act_alpha2')}
    del _L0_gnn_all

    def _L1_gnn_setup():
        import jax, jax.numpy as jnp
        import numpy as np
        N = 4096
        D = 512

        def adjacent_mat(adj):
            adj = adj + jnp.eye(adj.shape[0], dtype=adj.dtype)
            deg = jnp.sum(adj, axis=1)
            dinv = jnp.where(deg > 0, deg ** (-0.5), 0.0).astype(adj.dtype)
            return dinv[:, None] * adj * dinv[None, :]
        key = jax.random.key(seed)
        k1, k2 = jax.random.split(key)
        x = jax.random.normal(k1, (N, D), dtype=jnp.float32)
        Coefficient2 = 1e-08 * jnp.ones((N, N), dtype=jnp.float32)
        A = jax.random.uniform(k2, (N, N), dtype=jnp.float32)
        return {'x': x, 'Coefficient2': Coefficient2, 'A': A}
    _L1_gnn_all = _L1_gnn_setup()
    _L1_gnn_in = {k: v for k, v in _L1_gnn_all.items() if k in ()}
    del _L1_gnn_all
    return {'x': x, 'adj': adj, 'L0_gnn_adj_scaling_factor': _L0_gnn_in['adj_scaling_factor'], 'L0_gnn_weight': _L0_gnn_in['weight'], 'L0_gnn_wgt_alpha': _L0_gnn_in['wgt_alpha'], 'L0_gnn_act_alpha': _L0_gnn_in['act_alpha'], 'L0_gnn_act_alpha2': _L0_gnn_in['act_alpha2']}

def reference(x, adj, L0_gnn_adj_scaling_factor, L0_gnn_weight, L0_gnn_wgt_alpha, L0_gnn_act_alpha, L0_gnn_act_alpha2):
    import jax
    import jax.numpy as jnp

    def _L0_gnn_ref(input, adj, adj_scaling_factor, weight, wgt_alpha, act_alpha, act_alpha2):
        import jax, jax.numpy as jnp
        import numpy as np
        NBITS = 4
        N_NODES = 4096
        IN_F = 512
        OUT_F = 512

        def _act_quant(x, alpha, b):
            n = float(2 ** b - 1)
            xd = x / alpha
            xc = jnp.minimum(xd, 1.0)
            xq = jnp.round(xc * n) / n
            return xq * alpha

        def _weight_quant(w, alpha, b):
            n = float(2 ** b - 1)
            wd = w / alpha
            wc = jnp.clip(wd, -1.0, 1.0)
            wq = jnp.round(jnp.abs(wc) * n) / n * jnp.sign(wc)
            return wq * alpha
        bit = NBITS
        wb = bit - 1
        mean = jax.lax.stop_gradient(jnp.mean(weight))
        std = jax.lax.stop_gradient(jnp.std(weight, ddof=1))
        w_norm = (weight - mean) / std
        weight_q = _weight_quant(w_norm, wgt_alpha, wb)
        x = _act_quant(input, act_alpha, bit)
        wgt_delta = wgt_alpha / (2 ** (bit - 1) - 1)
        act_delta = act_alpha / (2 ** bit - 1)
        support = jnp.matmul(x / act_delta, weight_q / wgt_delta)
        support = support * act_delta * wgt_delta
        support = jax.nn.relu(support)
        support_q = _act_quant(support, act_alpha2, bit)
        support_delta = act_alpha2 / (2 ** bit - 1)
        output = jnp.matmul(adj / adj_scaling_factor, support_q / support_delta)
        return output * adj_scaling_factor * support_delta

    def _L1_gnn_ref(x, Coefficient2, A):
        import jax, jax.numpy as jnp
        import numpy as np
        N = 4096
        D = 512

        def adjacent_mat(adj):
            adj = adj + jnp.eye(adj.shape[0], dtype=adj.dtype)
            deg = jnp.sum(adj, axis=1)
            dinv = jnp.where(deg > 0, deg ** (-0.5), 0.0).astype(adj.dtype)
            return dinv[:, None] * adj * dinv[None, :]
        A_c = jax.lax.stop_gradient(A)
        adj = adjacent_mat((A_c + A_c.T) * 0.5)
        y = Coefficient2 @ adj
        y = y @ x
        return y
    x = _layernorm(x + _L0_gnn_ref(x, adj, L0_gnn_adj_scaling_factor, L0_gnn_weight, L0_gnn_wgt_alpha, L0_gnn_act_alpha, L0_gnn_act_alpha2), axis=-1)
    x = _layernorm(x + _L1_gnn_ref(x, adj, adj), axis=-1)
    return x

_drawn_inputs = setup_inputs


def setup_inputs(seed=0):
    import zlib

    import numpy as np

    out = dict(_drawn_inputs(seed))
    spreads = {}
    factors = {}
    for name, (base, spread) in spreads.items():
        noise = np.random.default_rng([zlib.crc32(name.encode()), seed]).standard_normal(out[name].shape)
        drawn = base * np.exp(spread * noise) if base else spread * noise
        out[name] = jnp.asarray(drawn.astype(out[name].dtype))
    for name, factor in factors.items():
        out[name] = (out[name] * factor).astype(out[name].dtype)
    return out
```

```python
from contextlib import ExitStack

import concourse.bass as bass
from concourse import mybir

F32 = mybir.dt.float32
F32R = mybir.dt.float32r
F16 = mybir.dt.float16
U8 = mybir.dt.uint8
I32 = mybir.dt.int32
ALU = mybir.AluOpType
ACT = mybir.ActivationFunctionType
AX = mybir.AxisListType
RMAX = bass.bass_isa.ReduceOp.max
RADD = bass.bass_isa.ReduceOp.add

P = 128
MAGIC = 1.5 * 2.0 ** 23
EXPONENT = 0x7F800000
TOP = 2.0 ** 14
ZS = 2.0 ** 11
US = 2.0 ** 5
EPS = 1e-5
BITS_A = 15.0
BITS_W = 7.0
SF, ALPHA_W, ALPHA_A, ALPHA_A2 = range(4)


def build(nc, x, adj, sf, weight, wgt_alpha, act_alpha, act_alpha2, out):
    N, F = x.shape
    NB = N // P
    FC = F // P
    J = 4
    NS = NB // J
    G = NB // 4
    H = NB // 2
    NZP = NB - J
    AT0 = 4
    LEAD = 3
    LN0 = 2
    RS0 = 1
    ST0 = 16
    WN = F * F

    x_blk = x.rearrange("(b p) f -> b p f", p=P)
    x_grp = x.rearrange("(g b p) f -> g p b f", p=P, b=4)
    adj_rows = adj.rearrange("(b p) c -> b p c", p=P)
    adj_half = adj.rearrange("(h k p) c -> h p k c", p=P, h=2)
    w_v = weight.rearrange("(c p) n -> p c n", p=P)
    out_blk = out.rearrange("(b p) f -> b p f", p=P)
    x1_d = nc.dram_tensor("x1_scratch", (NB, P, F), F32, kind="Internal").ap()
    u_d = nc.dram_tensor("u_scratch", (H, P, 2, F), F16, kind="Internal").ap()

    with ExitStack() as ctx:
        def sb(name, shape, dt):
            return ctx.enter_context(nc.sbuf_tensor(name, shape, dt))

        def sem(name):
            return ctx.enter_context(nc.semaphore(name))

        at_hi = sb("at_hi", [P, NB, N], F16)
        at_lo = sb("at_lo", [P, NB, N], F16)
        q_u = sb("q_u", [P, H, 2, F], F16)
        q_sb = q_u[:, :, :, :].rearrange("p k t f -> p (k t) f")
        nat = sb("nat", [P, J, N], F32)
        z = nat[:, :, :].rearrange("p j n -> p (j n)").bitcast(F16).rearrange(
            "p (k t f) -> p k t f", k=NB, t=2)
        xe = sb("xe", [P, 2, F], F32)
        ts = sb("ts", [P, 2, F], F32)
        x1t = sb("x1t", [P, 2, F], F32)
        u_st = x1t[:, 0, :].bitcast(F16).rearrange("p (t f) -> p t f", t=2)
        dump = sb("dump", [P, N], U8)
        ident = sb("ident", [P, P], F32)
        par = sb("par", [P, 4], F32)
        parb = sb("parb", [P, 4], F32)
        pinv = sb("pinv", [P, 4], F32)
        c1 = sb("c1", [P, 1], F32)
        k2 = sb("k2", [P, 1], F32)
        wst = sb("wst", [P, 8], F32)
        rmax = sb("rmax", [P, J], F32)
        rmx = sb("rmx", [P, 3], F32)
        cst = sb("cst", [P, 2], F32)
        pow2 = sb("pow2", [P, NS], F32)
        s_a = sb("s_a", [P, NS], F32)
        inv_a = sb("inv_a", [P, NS], F32)
        c2 = sb("c2", [P, NS], F32)
        c4 = sb("c4", [P, NS], F32)
        rowsum = sb("rowsum", [P, NB], F32)
        colsum = sb("colsum", [P, NB, NS], F32)
        deg = sb("deg", [P, NB], F32)
        degm = sb("degm", [P, NB], F32)
        dpow = sb("dpow", [P, NB], F32)
        dinv = sb("dinv", [P, NB], F32)
        dz = sb("dz", [P, NB], F32)
        eu = sb("eu", [P, NB], F32)
        nhalf = sb("nhalf", [P, NB], F32)
        bsc = sb("bsc", [P, 4], F32)
        bst = sb("bst", [P, 6], F32)
        mv = sb("mv", [P, 2, 2], F32)
        rv = sb("rv", [P, 2, 3], F32)

        with nc.sbuf_tensor("wi", [P, FC, F], F32R) as wi, nc.sbuf_tensor("xit", [P, 2, 2, F], F32R) as xit:
            pass
        sa = sb("sa", [P, 2, H, P], F32)
        bb = sb("bb", [P, 2, 2, H, P], F16)
        xz = bb[:, :, :, :, :].rearrange("p a t k c -> p (a t k c)").bitcast(F32).rearrange(
            "p (s f) -> p s f", s=4)
        xr = at_hi[:, :, N // 2:N].bitcast(F32)
        t1 = at_lo[:, 2:4, N // 2:N].bitcast(F32)
        wr = at_lo[:, 6:6 + FC, N // 2:N].bitcast(F32)

        ps = ctx.enter_context(nc.psum_tensor("ps", [P, 8, 512], F32))
        OUT, XT, TB = 0, 2, 4

        par_zero = sem("par_zero")
        ident_zero = sem("ident_zero")
        ident_done = sem("ident_done")
        consts = sem("consts")
        ld_par = sem("ld_par")
        ld_w = sem("ld_w")
        ld_x = [sem(f"ld_x{g}") for g in range(G)]
        ld_nat = [sem(f"ld_nat{j}") for j in range(J)]
        ld_xe = [sem(f"ld_xe{i}") for i in range(2)]
        ld_xz = [sem(f"ld_xz{i}") for i in range(4)]
        ld_sa = [sem(f"ld_sa{i}") for i in range(2)]
        ld_u = [sem(f"ld_u{i}") for i in range(H)]
        st_x1 = [sem(f"st_x1{i}") for i in range(2)]
        st_u = sem("st_u")
        par_all = sem("par_all")
        par_step = sem("par_step")
        w_step = sem("w_step")
        w_sum = sem("w_sum")
        w_tot = sem("w_tot")
        wi_done = sem("wi_done")
        x_clip = sem("x_clip")
        x_int = sem("x_int")
        xt_done = sem("xt_done")
        xh_done = sem("xh_done")
        xl_done = sem("xl_done")
        clip_done = sem("clip_done")
        q_done = sem("q_done")
        out_ready = sem("out_ready")
        out_free = sem("out_free")
        rmax_done = sem("rmax_done")
        rmx_part = sem("rmx_part")
        rmx_all = sem("rmx_all")
        rmx_copy = sem("rmx_copy")
        sc_step = sem("sc_step")
        sc_done = sem("sc_done")
        tb_ready = sem("tb_ready")
        ah_done = sem("ah_done")
        at_done = sem("at_done")
        rs_done = sem("rs_done")
        bs_done = sem("bs_done")
        mv_done = sem("mv_done")
        ve_done = sem("ve_done")
        rstd_done = sem("rstd_done")
        nmr_done = sem("nmr_done")
        ln_out = sem("ln_out")
        dg_step = sem("dg_step")
        dg_pow = sem("dg_pow")
        dg_done = sem("dg_done")
        zph = sem("zph")
        zp_done = sem("zp_done")
        zdh = sem("zdh")
        zd_done = sem("zd_done")
        add1 = sem("add1")
        add2 = sem("add2")
        diag = sem("diag")
        bh_done = sem("bh_done")
        b_done = sem("b_done")
        half_used = sem("half_used")
        uh_done = sem("uh_done")

        def bank(n):
            return ps[:, n % 2, :] if isinstance(n, int) else ps[:, bass.ds(n % 2, 1), :].rearrange("p a f -> p (a f)")

        N2, N3, N4 = NB, 2 * NB, 3 * NB
        block = ctx.enter_context(nc.Block())

        @block.sync
        def _(sp):
            sp.wait_ge(par_zero, 1)
            for i, a in enumerate((sf, wgt_alpha, act_alpha, act_alpha2)):
                sp.dma_start(par[0:1, i:i + 1], a.rearrange("(a b) -> a b", a=1)).then_inc(ld_par, 16)
            sp.dma_start(wr, w_v).then_inc(ld_w, 16)
            for g in range(G):
                sp.dma_start(xr[:, 4 * g:4 * g + 4, :], x_grp[g]).then_inc(ld_x[g], 16)
            for j in range(J):
                sp.dma_start(nat[:, j, :], adj_rows[j]).then_inc(ld_nat[j], 16)
            for i in range(2):
                sp.dma_start(xe[:, i, :], x_blk[i]).then_inc(ld_xe[i], 16)

            def store_x1(m, i):
                sp.wait_ge(ln_out, LN0 + m + 1)
                sp.dma_start(x1_d[m], x1t[:, i, :]).then_inc(st_x1[i], 16)

            def load_x(m, i):
                sp.wait_ge(out_free, N2 + m - 1)
                sp.dma_start(xe[:, i, :], x_blk[m]).then_inc(ld_xe[i], 16)

            with sp.Fori(0, NS - 1) as S:
                sp.wait_ge(at_done, AT0 + S * NB + NB)
                for j in range(J):
                    sp.wait_ge(rs_done, RS0 + S * J + j + 1)
                    sp.dma_start(nat[:, j, :], adj_rows[S * J + J + j]).then_inc(ld_nat[j], 16)
                for j in range(J):
                    load_x(S * J + j + 2, j % 2)
                    store_x1(S * J + j, j % 2)
            for h in range(2):
                sp.dma_start(sa[:, h, :, :], adj_half[h, :, :, 0:P]).then_inc(ld_sa[h], 16)
            for i in range(2):
                sp.wait_ge(st_x1[i], ST0 + 16 * (NZP // 2))
            for k in range(4):
                sp.dma_start(xz[:, k, :], x1_d[k]).then_inc(ld_xz[k], 16)
            for j in range(J):
                if j < 2:
                    load_x(NZP + j + 2, j % 2)
                store_x1(NZP + j, j % 2)
                if j < 2:
                    for i in range(4):
                        k = 4 * (j + 1) + i
                        sp.wait_ge(zp_done, k - 3)
                        sp.dma_start(xz[:, i, :], x1_d[k]).then_inc(ld_xz[i], 16)

            def load_half(i, h):
                sp.wait_ge(b_done, 2 * i + h - 1)
                sp.dma_start(sa[:, h, :, :], adj_half[h, :, :, bass.ts(i, P)]).then_inc(ld_sa[h], 16)

            with sp.Fori(1, H) as i:
                load_half(i, 0)
                load_half(i, 1)
            load_half(H, 0)
            load_half(H, 1)

            def store_u(i):
                sp.wait_ge(out_free, N3 + i + 1)
                sp.dma_start(u_d[i - H], u_st).then_inc(st_u, 16)

            with sp.Fori(H + 1, NB) as i:
                load_half(i, 0)
                load_half(i, 1)
                store_u(i - 1)
            for i in range(2):
                sp.wait_ge(st_x1[i], ST0 + 16 * (NB // 2))
                sp.dma_start(xe[:, i, :], x1_d[i]).then_inc(ld_xe[i], 16)
            sp.wait_ge(out_ready, N4)
            sp.wait_ge(st_u, ST0 + 16 * (H - 1))
            for k in range(H - 1):
                sp.dma_start(z[:, H + k, :, :], u_d[k]).then_inc(ld_u[k], 16)
            store_u(NB - 1)
            sp.wait_ge(st_u, ST0 + 16 * H)
            sp.dma_start(z[:, NB - 1, :, :], u_d[H - 1]).then_inc(ld_u[H - 1], 16)

            def final(m, b, i, more):
                sp.wait_ge(ln_out, LN0 + m + 1)
                sp.dma_start(out_blk[b], x1t[:, i, :]).then_inc(st_x1[i], 16)
                if more:
                    sp.wait_ge(out_free, N4 + b + 1)
                    sp.dma_start(xe[:, i, :], x1_d[b + 2]).then_inc(ld_xe[i], 16)

            with sp.Fori(0, NB // 2 - 1) as g:
                for i in range(2):
                    final(NB + 2 * g + i, 2 * g + i, i, True)
            for i in range(2):
                final(2 * NB - 2 + i, NB - 2 + i, i, False)
            for i in range(2):
                sp.wait_ge(st_x1[i], ST0 + 16 * NB)

        @block.gpsimd
        def _(pool):
            nc.gpsimd.memset(par[:, :], 0.0).then_inc(par_zero, 1)
            nc.gpsimd.memset(ident[:, :], 0.0).then_inc(ident_zero, 1)
            nc.gpsimd.memset(cst[:, 0:1], EPS).then_inc(consts, 1)
            nc.gpsimd.memset(cst[:, 1:2], 0.0).then_inc(consts, 1)
            nc.gpsimd.memset(nhalf[:, :], -0.5).then_inc(consts, 1)
            nc.gpsimd.memset(mv[:, :, :], 0.0).then_inc(ln_out, LN0)
            nc.gpsimd.memset(colsum[:, :, :], 0.0).then_inc(at_done, AT0)
            for i in range(2):
                nc.gpsimd.memset(rv[:, i, :], 0.0).then_inc(st_x1[i], ST0)
            nc.gpsimd.memset(rmx[:, :], 0.0).then_inc(st_u, ST0)
            pool.wait_ge(ident_zero, 1)
            nc.gpsimd.affine_select(out=ident[:, :], in_=ident[:, :], compare_op=ALU.not_equal, fill=1.0,
                                    base=0, pattern=[[-1, P]], channel_multiplier=1).then_inc(ident_done, 1)
            pool.wait_ge(ld_par, 64)
            nc.gpsimd.partition_all_reduce(parb[:, :], par[:, :], P, RADD).then_inc(par_all, 1)
            pool.wait_ge(w_sum, 1)
            nc.gpsimd.partition_all_reduce(wst[:, 1:2], wst[:, 0:1], P, RADD).then_inc(w_tot, 1)
            pool.wait_ge(rs_done, RS0)
            nc.gpsimd.partition_all_reduce(wst[:, 4:5], wst[:, 3:4], P, RADD).then_inc(w_tot, 1)
            pool.wait_ge(w_step, 3)
            pool.wait_ge(consts, 3)
            nc.gpsimd.tensor_tensor(wst[:, 6:7], wst[:, 5:6], nhalf[:, 0:1], ALU.pow).then_inc(w_tot, 1)
            for g in range(G):
                pool.wait_ge(x_clip, g + 1)
                v = xr[:, 4 * g:4 * g + 4, :]
                nc.gpsimd.tensor_scalar(v, v, BITS_A, MAGIC, ALU.mult, ALU.add).then_inc(x_int, 1)

            for b in range(NB):
                pool.wait_ge(clip_done, b + 1)
                nc.gpsimd.tensor_scalar(q_sb[:, b, :], t1[:, b % 2, :], 1.0, -MAGIC, ALU.mult, ALU.add).then_inc(q_done, 1)

            def largest(S):
                pool.wait_ge(rmx_part, S + 1)
                nc.gpsimd.tensor_tensor(rmx[:, 2:3], rmx[:, 0:1], cst[:, 1:2], ALU.add).then_inc(rmx_copy, 1)
                pool.wait_ge(consts, 3)
                pool.wait_ge(rmx_copy, S + 1)
                nc.gpsimd.partition_all_reduce(rmx[:, 1:2], rmx[:, 2:3], P, RMAX).then_inc(rmx_all, 1)

            largest(0)

            def rstd(m, i):
                pool.wait_ge(mv_done, m + 1)
                nc.gpsimd.tensor_tensor(rv[:, i, 0:1], mv[:, i, 1:2], cst[:, 0:1], ALU.add).then_inc(ve_done, 1)
                pool.wait_ge(ve_done, m + 1)
                nc.gpsimd.tensor_tensor(rv[:, i, 1:2], rv[:, i, 0:1], nhalf[:, 0:1], ALU.pow).then_inc(rstd_done, 1)
                pool.wait_ge(consts, 3)
                pool.wait_ge(rstd_done, m + 1)
                nc.gpsimd.tensor_scalar(rv[:, i, 2:3], mv[:, i, 0:1], rv[:, i, 1:2], -1.0,
                                        ALU.mult, ALU.mult).then_inc(nmr_done, 1)

            with pool.Fori(0, NS - 1) as S:
                for j in range(J - 1):
                    rstd(S * J + j, j % 2)
                largest(S + 1)
                rstd(S * J + J - 1, (J - 1) % 2)
            pool.wait_ge(dg_step, NS + 6)
            nc.gpsimd.tensor_tensor(dpow[:, :], degm[:, :], nhalf[:, :], ALU.pow).then_inc(dg_pow, 1)
            for j in range(J):
                rstd(NZP + j, j % 2)
            with pool.Fori(0, NB // 2) as g:
                for i in range(2):
                    rstd(NB + 2 * g + i, i)

        @block.scalar
        def _(act):
            act.wait_ge(w_step, 2)
            nc.scalar.activation(dump[:, :].rearrange("p (c n) -> p c n", c=FC), wr, ACT.Square,
                                 accum_out=wst[:, 3:4]).then_inc(rs_done, RS0)

            def x_hi(b, i):
                act.wait_ge(xt_done, b + 1)
                if not isinstance(b, int) or b >= 2:
                    act.wait_ge(out_ready, b - 1)
                nc.scalar.activation(xit[:, i, 0, :], ps[:, XT + i, :], ACT.Copy, bias=-MAGIC).then_inc(xh_done, 1)

            def relu(b, i):
                act.wait_ge(out_ready, b + 1)
                if not isinstance(b, int) or b >= 2:
                    act.wait_ge(q_done, b - 1)
                else:
                    act.wait_ge(par_step, 4)
                nc.scalar.activation(t1[:, i, :], ps[:, OUT + i, :], ACT.Relu, scale=c1[:, 0:1]).then_inc(out_free, 1)

            x_hi(0, 0)
            x_hi(1, 1)
            relu(0, 0)
            with act.Fori(1, NB // 2) as g:
                x_hi(2 * g, 0)
                relu(2 * g - 1, 1)
                x_hi(2 * g + 1, 1)
                relu(2 * g, 0)
            relu(NB - 1, 1)

            def at_high(S, k):
                act.wait_ge(tb_ready, S * NB + k + 1)
                nc.scalar.activation(at_hi[:, k, bass.ts(S, J * P)], ps[:, TB + k % 4, :], ACT.Copy,
                                     scale=s_a[:, bass.ds(S, 1)],
                                     accum_out=colsum[:, k, bass.ds(S, 1)]).then_inc(ah_done, 1)

            def sum_rows(S, j):
                act.wait_ge(ld_nat[j], 16 * S + 16)
                act.wait_ge(rs_done, RS0 + S * J + j)
                nc.scalar.activation(dump[:, :], nat[:, j, :], ACT.Copy,
                                     accum_out=rowsum[:, bass.ds(S * J + j, 1)]).then_inc(rs_done, 1)

            def normalise(m, i, used):
                act.wait_ge(nmr_done, m + 1)
                act.wait_ge(st_x1[i], used)
                nc.scalar.activation(x1t[:, i, :], ts[:, i, :], ACT.Identity, scale=rv[:, i, 1:2],
                                     bias=rv[:, i, 2:3]).then_inc(ln_out, 1)

            with act.Fori(0, NS - 1) as S:
                act.wait_ge(sc_done, S + 1)
                for k in range(NB):
                    at_high(S, k)
                sum_rows(S, 0)
                sum_rows(S, 1)
                for j in range(J):
                    normalise(S * J + j, j % 2, ST0 + 32 * S + 16 * (j // 2))
                    if j == 0:
                        sum_rows(S, 2)
                        sum_rows(S, 3)
            act.wait_ge(sc_done, NS)
            for k in range(NB):
                at_high(NS - 1, k)
            for j in range(J):
                sum_rows(NS - 1, j)

            def z_back(k):
                act.wait_ge(ld_xz[k % 4], 16 * (k // 4) + 16)
                nc.scalar.activation(z[:, k, 0, :], xz[:, k % 4, :], ACT.Copy, scale=dz[:, k:k + 1]).then_inc(zph, 1)

            def z_here(j):
                k = NZP + j
                act.wait_ge(ln_out, LN0 + k + 1)
                nc.scalar.activation(z[:, k, 0, :], x1t[:, j % 2, :], ACT.Copy, scale=dz[:, k:k + 1]).then_inc(zdh, 1)

            def last_norm(j):
                if j >= 2:
                    act.wait_ge(zd_done, j - 1)
                normalise(NZP + j, j % 2, ST0 + 16 * ((NZP + j) // 2))

            def b_high(i, h, diagonal):
                if diagonal:
                    act.wait_ge(diag, i + 1)
                else:
                    act.wait_ge(add2, 2 * i + h + 1)
                if not isinstance(i, int) or i > 0:
                    if h == 0:
                        act.wait_ge(half_used, i)
                    else:
                        act.wait_ge(out_ready, N3 + i)
                nc.scalar.activation(bb[:, h, 0, :, :], sa[:, h, :, :], ACT.Copy, scale=bsc[:, 2:3]).then_inc(bh_done, 1)

            def u_high(i, dst):
                act.wait_ge(out_ready, N3 + i + 1)
                nc.scalar.activation(dst, bank(i), ACT.Copy, scale=eu[:, bass.ds(i, 1)]).then_inc(uh_done, 1)

            def u_staged(i):
                act.wait_ge(st_u, 16 * (i - H) + 16)
                u_high(i, u_st[:, 0, :])

            last_norm(0)
            act.wait_ge(dg_done, 1)
            act.wait_ge(at_done, AT0 + NS * NB)
            for k in range(0, 4):
                z_back(k)
            last_norm(1)
            z_here(0)
            for k in range(4, 8):
                z_back(k)
            last_norm(2)
            z_here(1)
            for k in range(8, NZP):
                z_back(k)
            z_here(2)
            act.wait_ge(zp_done, NZP)
            b_high(0, 0, True)
            b_high(0, 1, False)
            last_norm(3)
            z_here(3)
            with act.Fori(1, H) as i:
                b_high(i, 0, True)
                u_high(i - 1, q_u[:, bass.ds(i - 1, 1), 0, :].rearrange("p a f -> p (a f)"))
                b_high(i, 1, False)
            b_high(H, 0, False)
            u_high(H - 1, q_u[:, H - 1, 0, :])
            b_high(H, 1, True)
            act.wait_ge(zd_done, J)
            act.wait_ge(st_x1[0], ST0 + 16 * (NB // 2))
            with act.Fori(H + 1, NB) as i:
                b_high(i, 0, False)
                u_staged(i - 1)
                b_high(i, 1, True)
            u_staged(NB - 1)
            act.wait_ge(st_u, 16 * H + ST0)
            with act.Fori(0, NB // 2) as g:
                for i in range(2):
                    normalise(NB + 2 * g + i, i, ST0 + 16 * (NB // 2) + 16 * g)

        @block.vector
        def _(dve):
            def step(s, n, ins):
                ins.then_inc(s, 1)
                dve.wait_ge(s, n)

            dve.wait_ge(ld_w, 16)
            nc.vector.tensor_reduce(wst[:, 0:1], wr, AX.XY, ALU.add).then_inc(w_sum, 1)
            dve.wait_ge(par_all, 1)
            step(par_step, 1, nc.vector.reciprocal(pinv[:, :], parb[:, :]))
            nc.vector.tensor_scalar(c1[:, :], parb[:, ALPHA_A:ALPHA_A + 1], 1.0 / BITS_A,
                                    parb[:, ALPHA_W:ALPHA_W + 1], ALU.mult, ALU.mult).then_inc(par_step, 1)
            nc.vector.tensor_scalar(k2[:, :], parb[:, ALPHA_A2:ALPHA_A2 + 1], 1.0 / BITS_A,
                                    parb[:, SF:SF + 1], ALU.mult, ALU.mult).then_inc(par_step, 1)
            dve.wait_ge(par_step, 3)
            nc.vector.tensor_scalar(c1[:, :], c1[:, :], pinv[:, ALPHA_A2:ALPHA_A2 + 1], BITS_A / BITS_W,
                                    ALU.mult, ALU.mult).then_inc(par_step, 1)
            nc.vector.tensor_scalar(k2[:, :], k2[:, :], pinv[:, SF:SF + 1], None, ALU.mult).then_inc(par_step, 1)
            dve.wait_ge(w_tot, 1)
            step(w_step, 1, nc.vector.tensor_scalar(wst[:, 2:3], wst[:, 1:2], -1.0 / WN, None, ALU.mult))
            step(w_step, 2, nc.vector.tensor_scalar(wr, wr, wst[:, 2:3], None, ALU.add))

            def clip_x(g):
                dve.wait_ge(ld_x[g], 16)
                v = xr[:, 4 * g:4 * g + 4, :]
                nc.vector.tensor_scalar(v, v, pinv[:, ALPHA_A:ALPHA_A + 1], 1.0, ALU.mult, ALU.min).then_inc(x_clip, 1)

            dve.wait_ge(w_tot, 2)
            nc.vector.tensor_scalar(wst[:, 5:6], wst[:, 4:5], 1.0 / (WN - 1), None, ALU.mult).then_inc(w_step, 1)
            clip_x(0)
            dve.wait_ge(w_tot, 3)
            step(w_step, 4, nc.vector.tensor_scalar(wst[:, 7:8], wst[:, 6:7], pinv[:, ALPHA_W:ALPHA_W + 1], None, ALU.mult))
            step(w_step, 5, nc.vector.tensor_scalar(wr, wr, wst[:, 7:8], 1.0, ALU.mult, ALU.min))
            step(w_step, 6, nc.vector.tensor_scalar(wr, wr, -1.0, BITS_W, ALU.max, ALU.mult))
            nc.vector.tensor_scalar(wi[:, :, :], wr, MAGIC, -MAGIC, ALU.add, ALU.add).then_inc(wi_done, 1)
            for g in range(1, G):
                clip_x(g)

            def x_lo(b, i):
                dve.wait_ge(xh_done, b + 1)
                nc.vector.scalar_tensor_tensor(out=xit[:, i, 1, :], in0=ps[:, XT + i, :], scalar=-MAGIC,
                                               in1=xit[:, i, 0, :].bitcast(F32), op0=ALU.add,
                                               op1=ALU.subtract).then_inc(xl_done, 1)

            def clip(b, i):
                dve.wait_ge(out_free, b + 1)
                nc.vector.tensor_scalar(t1[:, i, :], t1[:, i, :], BITS_A, MAGIC, ALU.min, ALU.add).then_inc(clip_done, 1)

            x_lo(0, 0)
            x_lo(1, 1)
            clip(0, 0)
            with dve.Fori(1, NB // 2) as g:
                x_lo(2 * g, 0)
                clip(2 * g - 1, 1)
                x_lo(2 * g + 1, 1)
                clip(2 * g, 0)
            clip(NB - 1, 1)

            def row_max(S, j):
                dve.wait_ge(ld_nat[j], 16 * S + 16)
                nc.vector.tensor_reduce(rmax[:, j:j + 1], nat[:, j, :], AX.X, ALU.max,
                                        apply_absolute_value=True).then_inc(rmax_done, 1)

            def scales(S):
                def col(t):
                    return t[:, bass.ds(S, 1)]
                dve.wait_ge(rmax_done, J * S + J)
                nc.vector.tensor_reduce(rmx[:, 0:1], rmax[:, :], AX.X, ALU.max).then_inc(rmx_part, 1)
                dve.wait_ge(rmx_all, S + 1)
                step(sc_step, 2 * S + 1, nc.vector.tensor_scalar(
                    col(pow2).bitcast(I32), rmx[:, 1:2].bitcast(I32), EXPONENT, None, ALU.bitwise_and))
                step(sc_step, 2 * S + 2, nc.vector.tensor_scalar(
                    col(inv_a), col(pow2), 2.0 ** -100, 1.0 / TOP, ALU.max, ALU.mult))
                nc.vector.reciprocal(col(s_a), col(inv_a))
                nc.vector.tensor_scalar(col(c2), col(inv_a), k2[:, 0:1], None, ALU.mult)
                nc.vector.tensor_scalar(col(c4), col(inv_a), 1.0 / US, None, ALU.mult).then_inc(sc_done, 1)

            def at_low(S, k):
                dve.wait_ge(ah_done, S * NB + k + 1)
                nc.vector.scalar_tensor_tensor(out=at_lo[:, k, bass.ts(S, J * P)], in0=ps[:, TB + k % 4, :],
                                               scalar=s_a[:, bass.ds(S, 1)], in1=at_hi[:, k, bass.ts(S, J * P)],
                                               op0=ALU.mult, op1=ALU.subtract).then_inc(at_done, 1)

            def moments(m, n, i, scale):
                dve.wait_ge(out_ready, n + 1)
                dve.wait_ge(ld_xe[i], 16 * (m // 2) + 16)
                dve.wait_ge(ln_out, LN0 + m - 1)
                nc.vector.scalar_tensor_tensor(out=ts[:, i, :], in0=ps[:, OUT + i, :], scalar=scale,
                                               in1=xe[:, i, :], op0=ALU.mult, op1=ALU.add).then_inc(out_free, 1)
                dve.wait_ge(out_free, n + 1)
                nc.vector.bn_stats(bst[:, :], ts[:, i, :]).then_inc(bs_done, 1)
                dve.wait_ge(consts, 3)
                dve.wait_ge(bs_done, m + 1)
                nc.vector.bn_aggr(mv[:, i, :], bst[:, :]).then_inc(mv_done, 1)

            for j in range(J):
                row_max(0, j)
            scales(0)
            with dve.Fori(0, NS - 1) as S:
                for k in range(NB):
                    at_low(S, k)
                for j in range(J):
                    if j == J - 1:
                        for jj in range(J):
                            row_max(S + 1, jj)
                        scales(S + 1)
                    moments(S * J + j, N2 + S * J + j, j % 2, c2[:, bass.ds(S, 1)])
            for k in range(NB):
                at_low(NS - 1, k)

            step(dg_step, 1, nc.vector.tensor_reduce(bsc[:, 0:1], pow2[:, :], AX.X, ALU.max))
            step(dg_step, 2, nc.vector.tensor_scalar(bsc[:, 0:1], bsc[:, 0:1], 4.0, 2.0, ALU.mult, ALU.add))
            step(dg_step, 3, nc.vector.tensor_scalar(bsc[:, 3:4].bitcast(I32), bsc[:, 0:1].bitcast(I32),
                                                     EXPONENT, None, ALU.bitwise_and))
            step(dg_step, 4, nc.vector.tensor_scalar(bsc[:, 1:2], bsc[:, 3:4], 1.0 / TOP, None, ALU.mult))
            nc.vector.reciprocal(bsc[:, 2:3], bsc[:, 1:2])
            for S in range(NS):
                if S == 0:
                    dve.wait_ge(rs_done, RS0 + NB)
                nc_in1 = rowsum[:, :] if S == 0 else deg[:, :]
                step(dg_step, 5 + S, nc.vector.scalar_tensor_tensor(
                    out=deg[:, :], in0=colsum[:, :, S], scalar=inv_a[:, S:S + 1], in1=nc_in1,
                    op0=ALU.mult, op1=ALU.add))
            step(dg_step, 9, nc.vector.tensor_scalar(deg[:, :], deg[:, :], 0.5, 1.0, ALU.mult, ALU.add))
            nc.vector.tensor_scalar(degm[:, :], deg[:, :], 1e-30, None, ALU.max).then_inc(dg_step, 1)
            moments(NZP, N2 + NZP, 0, c2[:, NS - 1:NS])
            dve.wait_ge(dg_pow, 1)
            step(dg_step, 11, nc.vector.scalar_tensor_tensor(out=dinv[:, :], in0=deg[:, :], scalar=0.0,
                                                             in1=dpow[:, :], op0=ALU.is_gt, op1=ALU.mult))
            nc.vector.tensor_scalar(eu[:, :], dinv[:, :], bsc[:, 1:2], 0.5 * US / ZS, ALU.mult, ALU.mult)
            step(dg_done, 1, nc.vector.tensor_scalar(dz[:, :], dinv[:, :], ZS, None, ALU.mult))

            def z_back(k):
                dve.wait_ge(zph, k + 1)
                nc.vector.scalar_tensor_tensor(out=z[:, k, 1, :], in0=xz[:, k % 4, :], scalar=dz[:, k:k + 1],
                                               in1=z[:, k, 0, :], op0=ALU.mult, op1=ALU.subtract).then_inc(zp_done, 1)

            def z_here(j):
                k = NZP + j
                dve.wait_ge(zdh, j + 1)
                nc.vector.scalar_tensor_tensor(out=z[:, k, 1, :], in0=x1t[:, j % 2, :], scalar=dz[:, k:k + 1],
                                               in1=z[:, k, 0, :], op0=ALU.mult, op1=ALU.subtract).then_inc(zd_done, 1)

            def add_half(i, h, diagonal):
                n = 2 * i + h
                S = i // J
                inv = inv_a[:, bass.ds(S, 1)]
                dve.wait_ge(ld_sa[h], 16 * i + 16)
                nc.vector.scalar_tensor_tensor(out=sa[:, h, :, :], in0=at_hi[:, H * h:H * h + H, bass.ts(i, P)],
                                               scalar=inv, in1=sa[:, h, :, :], op0=ALU.mult,
                                               op1=ALU.add).then_inc(add1, 1)
                dve.wait_ge(add1, n + 1)
                nc.vector.scalar_tensor_tensor(out=sa[:, h, :, :], in0=at_lo[:, H * h:H * h + H, bass.ts(i, P)],
                                               scalar=inv, in1=sa[:, h, :, :], op0=ALU.mult,
                                               op1=ALU.add).then_inc(add2, 1)
                if diagonal:
                    dve.wait_ge(add2, n + 1)
                    d = sa[:, h, bass.ds(i - H * h, 1), :].rearrange("p a c -> p (a c)")
                    nc.vector.scalar_tensor_tensor(out=d, in0=ident[:, :], scalar=2.0, in1=d, op0=ALU.mult,
                                                   op1=ALU.add).then_inc(diag, 1)

            def b_low(i, h):
                dve.wait_ge(bh_done, 2 * i + h + 1)
                nc.vector.scalar_tensor_tensor(out=bb[:, h, 1, :, :], in0=sa[:, h, :, :], scalar=bsc[:, 2:3],
                                               in1=bb[:, h, 0, :, :], op0=ALU.mult,
                                               op1=ALU.subtract).then_inc(b_done, 1)

            def u_low(i, hi, lo):
                dve.wait_ge(uh_done, i + 1)
                nc.vector.scalar_tensor_tensor(out=lo, in0=bank(i), scalar=eu[:, bass.ds(i, 1)], in1=hi,
                                               op0=ALU.mult, op1=ALU.subtract).then_inc(out_free, 1)

            for k in range(0, 4):
                z_back(k)
            moments(NZP + 1, N2 + NZP + 1, 1, c2[:, NS - 1:NS])
            z_here(0)
            for k in range(4, 8):
                z_back(k)
            moments(NZP + 2, N2 + NZP + 2, 0, c2[:, NS - 1:NS])
            z_here(1)
            for k in range(8, NZP):
                z_back(k)
            z_here(2)
            add_half(0, 0, True)
            add_half(0, 1, False)
            b_low(0, 0)
            b_low(0, 1)
            moments(NB - 1, N2 + NB - 1, 1, c2[:, NS - 1:NS])
            z_here(3)

            def strip(i, first, hi, lo):
                add_half(i, 0, first)
                add_half(i, 1, not first)
                b_low(i, 0)
                u_low(i - 1, hi, lo)
                b_low(i, 1)

            def u_block(i, t):
                return q_u[:, bass.ds(i, 1), t, :].rearrange("p a f -> p (a f)")

            with dve.Fori(1, H) as i:
                strip(i, True, u_block(i - 1, 0), u_block(i - 1, 1))
            strip(H, False, q_u[:, H - 1, 0, :], q_u[:, H - 1, 1, :])
            with dve.Fori(H + 1, NB) as i:
                strip(i, False, u_st[:, 0, :], u_st[:, 1, :])
            u_low(NB - 1, u_st[:, 0, :], u_st[:, 1, :])
            with dve.Fori(0, NS) as S:
                for j in range(J):
                    moments(NB + S * J + j, N4 + S * J + j, j % 2, c4[:, bass.ds(S, 1)])

        @block.tensor
        def _(pe):
            pe.wait_ge(ident_done, 1)

            def turn_x(b):
                if b % 4 == 0:
                    pe.wait_ge(x_int, b // 4 + 1)
                if b >= 2:
                    pe.wait_ge(xl_done, b - 1)
                for c in range(FC):
                    mm = nc.tensor.transpose(ps[:, XT + b % 2, c * P:(c + 1) * P], xr[:, b, c * P:(c + 1) * P],
                                             ident[:, :])
                mm.then_inc(xt_done, 1)

            def times_w(b):
                pe.wait_ge(xl_done, b + 1)
                if b == 0:
                    pe.wait_ge(wi_done, 1)
                if b >= 2:
                    pe.wait_ge(out_free, b - 1)
                for c in range(FC):
                    for t in range(2):
                        mm = nc.tensor.matmul(ps[:, OUT + b % 2, :], xit[:, b % 2, t, c * P:(c + 1) * P],
                                              wi[:, c, :], start=(c + t == 0), stop=(c == FC - 1 and t == 1))
                mm.then_inc(out_ready, 1)

            turn_x(0)
            for b in range(NB):
                if b + 1 < NB:
                    turn_x(b + 1)
                times_w(b)

            def turn_adj(S, k):
                pe.wait_ge(at_done, S * NB + k + 1)
                for j in range(J):
                    if k == 0:
                        pe.wait_ge(ld_nat[j], 16 * S + 16)
                    mm = nc.tensor.transpose(ps[:, TB + k % 4, j * P:(j + 1) * P], nat[:, j, k * P:(k + 1) * P],
                                             ident[:, :])
                mm.then_inc(tb_ready, 1)

            with pe.Fori(0, NS) as S:
                for k in range(LEAD):
                    turn_adj(S, k)
                for j in range(J):
                    pe.wait_ge(out_free, N2 + S * J + j - 1)
                    for k in range(NB):
                        if j == 0:
                            if k + LEAD < NB:
                                turn_adj(S, k + LEAD)
                            pe.wait_ge(at_done, AT0 + S * NB + k + 1)
                            if k == 0:
                                pe.wait_ge(q_done, NB)
                        for a in (at_hi, at_lo):
                            mm = nc.tensor.matmul(ps[:, OUT + j % 2, :], a[:, k, bass.ts(S * J + j, P)],
                                                  q_sb[:, k, :], start=(k == 0 and a is at_hi),
                                                  stop=(k == NB - 1 and a is at_lo))
                    mm.then_inc(out_ready, 1)

            def times_z(i):
                pe.wait_ge(out_free, N3 + i - 1)
                for h in range(2):
                    pe.wait_ge(b_done, 2 * i + h + 1)
                    for kk in range(H):
                        k = h * H + kk
                        if isinstance(i, int) and k >= NZP:
                            pe.wait_ge(zd_done, k - NZP + 1)
                        for a, t in ((0, 0), (0, 1), (1, 0)):
                            mm = nc.tensor.matmul(bank(i), bb[:, h, a, kk, :], z[:, k, t, :],
                                                  start=(k == 0 and a + t == 0), stop=(k == NB - 1 and a == 1))
                    mm.then_inc(half_used if h == 0 else out_ready, 1)

            times_z(0)
            with pe.Fori(1, NB) as i:
                times_z(i)

            def times_u(g, first):
                for i in range(2):
                    pe.wait_ge(out_free, N4 + 2 * g + i - 1)
                    for k in range(NB):
                        if first and i == 0:
                            if k < H:
                                pe.wait_ge(out_free, N3 + k + 1)
                            else:
                                pe.wait_ge(ld_u[k - H], 16)
                        u = q_u[:, k, :, :] if k < H else z[:, k, :, :]
                        for a, t in ((at_hi, 0), (at_hi, 1), (at_lo, 0)):
                            mm = nc.tensor.matmul(ps[:, OUT + i, :], a[:, k, bass.ts(2 * g + i, P)], u[:, t, :],
                                                  start=(k == 0 and a is at_hi and t == 0),
                                                  stop=(k == NB - 1 and a is at_lo))
                    mm.then_inc(out_ready, 1)

            times_u(0, True)
            with pe.Fori(1, NB // 2) as g:
                times_u(g, False)


_INS = ["x", "adj", "L0_gnn_adj_scaling_factor", "L0_gnn_weight", "L0_gnn_wgt_alpha", "L0_gnn_act_alpha",
        "L0_gnn_act_alpha2"]


def kernel(**inputs):
    import numpy as _np
    import concourse.bacc as _bacc
    from concourse import mybir as _mybir
    from concourse.bass_utils import run_bass_kernel_spmd as _run

    nc = _bacc.Bacc("TRN2", target_bir_lowering=False, num_devices=1)
    arrays, args = {}, []
    for name in _INS:
        a = _np.ascontiguousarray(inputs[name])
        arrays[f"in_{name}_dram"] = a
        args.append(nc.dram_tensor(f"in_{name}_dram", a.shape, _mybir.dt.from_np(a.dtype), kind="ExternalInput").ap())
    args.append(nc.dram_tensor("out_0_dram", inputs["x"].shape, _mybir.dt.float32, kind="ExternalOutput").ap())
    build(nc, *args)
    r = _run(nc, [arrays], core_ids=[0])
    return r.results[0]["out_0_dram"]
```

```python
from contextlib import ExitStack

import concourse.bass as bass
from concourse import mybir

F32 = mybir.dt.float32
F32R = mybir.dt.float32r
F16 = mybir.dt.float16
U8 = mybir.dt.uint8
I32 = mybir.dt.int32
ALU = mybir.AluOpType
ACT = mybir.ActivationFunctionType
AX = mybir.AxisListType
RMAX = bass.bass_isa.ReduceOp.max
RADD = bass.bass_isa.ReduceOp.add

P = 128
MAGIC = 1.5 * 2.0 ** 23
EXPONENT = 0x7F800000
TOP = 2.0 ** 14
ZS = 2.0 ** 11
US = 2.0 ** 5
EPS = 1e-5
BITS_A = 15.0
BITS_W = 7.0
SF, ALPHA_W, ALPHA_A, ALPHA_A2 = range(4)


def build(nc, x, adj, sf, weight, wgt_alpha, act_alpha, act_alpha2, out):
    N, F = x.shape
    NB = N // P
    FC = F // P
    J = 4
    NS = NB // J
    G = NB // 4
    H = NB // 2
    NZP = NB - J
    AT0 = 4
    LEAD = 4
    G0 = 3
    LN0 = 2
    RS0 = 1
    ST0 = 16
    WN = F * F

    x_blk = x.rearrange("(b p) f -> b p f", p=P)
    x_grp = x.rearrange("(g b p) f -> g p b f", p=P, b=4)
    adj_rows = adj.rearrange("(b p) c -> b p c", p=P)
    adj_half = adj.rearrange("(h k p) c -> h p k c", p=P, h=2)
    w_v = weight.rearrange("(c p) n -> p c n", p=P)
    out_blk = out.rearrange("(b p) f -> b p f", p=P)
    x1_d = nc.dram_tensor("x1_scratch", (NB, P, F), F32, kind="Internal").ap()
    u_d = nc.dram_tensor("u_scratch", (H, P, 2, F), F16, kind="Internal").ap()

    with ExitStack() as ctx:
        def sb(name, shape, dt):
            return ctx.enter_context(nc.sbuf_tensor(name, shape, dt))

        def sem(name):
            return ctx.enter_context(nc.semaphore(name))

        at_hi = sb("at_hi", [P, NB, N], F16)
        at_lo = sb("at_lo", [P, NB, N], F16)
        q_u = sb("q_u", [P, H, 2, F], F16)
        q_sb = q_u[:, :, :, :].rearrange("p k t f -> p (k t) f")
        nat = sb("nat", [P, J, N], F32)
        z = nat[:, :, :].rearrange("p j n -> p (j n)").bitcast(F16).rearrange(
            "p (k t f) -> p k t f", k=NB, t=2)
        xe = sb("xe", [P, 2, F], F32)
        ts = sb("ts", [P, 2, F], F32)
        x1t = sb("x1t", [P, 2, F], F32)
        u_st = x1t[:, 0, :].bitcast(F16).rearrange("p (t f) -> p t f", t=2)
        dump = sb("dump", [P, N], U8)
        wbn = dump[:, 0:24 * FC].bitcast(F32).rearrange("p (c s) -> p c s", c=FC)
        ident = sb("ident", [P, P], F32)
        par = sb("par", [P, 4], F32)
        parb = sb("parb", [P, 4], F32)
        pinv = sb("pinv", [P, 4], F32)
        c1 = sb("c1", [P, 1], F32)
        k2 = sb("k2", [P, 1], F32)
        wst = sb("wst", [P, 8], F32)
        rmax = sb("rmax", [P, 2 * J], F32)
        rmx = sb("rmx", [P, 3], F32)
        cst = sb("cst", [P, 2], F32)
        pow2 = sb("pow2", [P, NS], F32)
        s_a = sb("s_a", [P, NS], F32)
        inv_a = sb("inv_a", [P, NS], F32)
        c2 = sb("c2", [P, NS], F32)
        c4 = sb("c4", [P, NS], F32)
        rowsum = sb("rowsum", [P, NB], F32)
        colsum = sb("colsum", [P, NB, NS], F32)
        deg = sb("deg", [P, NB], F32)
        degm = sb("degm", [P, NB], F32)
        dpow = sb("dpow", [P, NB], F32)
        dinv = sb("dinv", [P, NB], F32)
        dz = sb("dz", [P, NB], F32)
        eu = sb("eu", [P, NB], F32)
        nhalf = sb("nhalf", [P, NB], F32)
        bsc = sb("bsc", [P, 4], F32)
        bst = sb("bst", [P, 6], F32)
        mv = sb("mv", [P, 2, 2], F32)
        rv = sb("rv", [P, 2, 3], F32)

        with nc.sbuf_tensor("wi", [P, FC, F], F32R) as wi, nc.sbuf_tensor("xit", [P, 2, 2, F], F32R) as xit:
            pass
        sa = sb("sa", [P, 2, H, P], F32)
        bb = sb("bb", [P, 2, 2, H, P], F16)
        xz = bb[:, :, :, :, :].rearrange("p a t k c -> p (a t k c)").bitcast(F32).rearrange(
            "p (s f) -> p s f", s=4)
        xr = at_hi[:, :, N // 2:N].bitcast(F32)
        t1 = at_lo[:, 2:4, N // 2:N].bitcast(F32)
        wr = at_lo[:, 6:6 + FC, N // 2:N].bitcast(F32)

        ps = ctx.enter_context(nc.psum_tensor("ps", [P, 8, 512], F32))
        OUT, XT, TB = 0, 2, 4

        par_zero = sem("par_zero")
        ident_zero = sem("ident_zero")
        ident_done = sem("ident_done")
        consts = sem("consts")
        ld_par = sem("ld_par")
        ld_w = [sem(f"ld_w{c}") for c in range(FC)]
        ld_x = [sem(f"ld_x{g}") for g in range(G)]
        ld_nat = [sem(f"ld_nat{j}") for j in range(J)]
        ld_xe = [sem(f"ld_xe{i}") for i in range(2)]
        ld_xz = [sem(f"ld_xz{i}") for i in range(4)]
        ld_sa = [sem(f"ld_sa{i}") for i in range(2)]
        ld_u = [sem(f"ld_u{i}") for i in range(H)]
        st_x1 = [sem(f"st_x1{i}") for i in range(2)]
        st_u = sem("st_u")
        par_all = sem("par_all")
        par_step = sem("par_step")
        w_step = sem("w_step")
        w_stat = sem("w_stat")
        w_mom = sem("w_mom")
        w_tot = sem("w_tot")
        wi_done = sem("wi_done")
        x_clip = sem("x_clip")
        x_int = sem("x_int")
        xt_done = sem("xt_done")
        xh_done = sem("xh_done")
        xl_done = sem("xl_done")
        clip_done = sem("clip_done")
        q_done = sem("q_done")
        out_ready = sem("out_ready")
        out_free = sem("out_free")
        rmax_done = sem("rmax_done")
        rmx_part = sem("rmx_part")
        rmx_all = sem("rmx_all")
        rmx_copy = sem("rmx_copy")
        sc_step = sem("sc_step")
        sc_done = sem("sc_done")
        tb_ready = sem("tb_ready")
        ah_done = sem("ah_done")
        at_done = sem("at_done")
        rs_done = sem("rs_done")
        bs_done = sem("bs_done")
        mv_done = sem("mv_done")
        ve_done = sem("ve_done")
        rstd_done = sem("rstd_done")
        nmr_done = sem("nmr_done")
        ln_out = sem("ln_out")
        dg_step = sem("dg_step")
        dg_pow = sem("dg_pow")
        dg_done = sem("dg_done")
        zph = sem("zph")
        zp_done = sem("zp_done")
        zdh = sem("zdh")
        zd_done = sem("zd_done")
        add1 = sem("add1")
        add2 = sem("add2")
        diag = sem("diag")
        bh_done = sem("bh_done")
        b_done = sem("b_done")
        half_used = sem("half_used")
        uh_done = sem("uh_done")

        def bank(n):
            return ps[:, n % 2, :] if isinstance(n, int) else ps[:, bass.ds(n % 2, 1), :].rearrange("p a f -> p (a f)")

        N2, N3, N4 = NB, 2 * NB, 3 * NB
        block = ctx.enter_context(nc.Block())

        @block.sync
        def _(sp):
            for c in range(FC):
                sp.dma_start(wr[:, c, :], w_v[:, c, :]).then_inc(ld_w[c], 16)
            sp.wait_ge(par_zero, 1)
            for i, a in enumerate((sf, wgt_alpha, act_alpha, act_alpha2)):
                sp.dma_start(par[0:1, i:i + 1], a.rearrange("(a b) -> a b", a=1)).then_inc(ld_par, 16)
            for g in range(G):
                sp.dma_start(xr[:, 4 * g:4 * g + 4, :], x_grp[g]).then_inc(ld_x[g], 16)
            for j in range(J):
                sp.dma_start(nat[:, j, :], adj_rows[j]).then_inc(ld_nat[j], 16)
            for i in range(2):
                sp.dma_start(xe[:, i, :], x_blk[i]).then_inc(ld_xe[i], 16)

            def store_x1(m, i):
                sp.wait_ge(ln_out, LN0 + m + 1)
                sp.dma_start(x1_d[m], x1t[:, i, :]).then_inc(st_x1[i], 16)

            def load_x(m, i):
                sp.wait_ge(out_free, N2 + m - 1)
                sp.dma_start(xe[:, i, :], x_blk[m]).then_inc(ld_xe[i], 16)

            def superblock(S, first):
                sp.wait_ge(at_done, AT0 + S * NB + NB)
                for j in range(J):
                    sp.wait_ge(rs_done, RS0 + S * J + j + 1)
                    sp.dma_start(nat[:, j, :], adj_rows[S * J + J + j]).then_inc(ld_nat[j], 16)
                for j in range(J - 1):
                    load_x(S * J + j + 2, j % 2)
                    store_x1(S * J + j, j % 2)
                load_x(S * J + J + 1, 1)
                store_x1(S * J + J - 1, 1)

            superblock(0, True)
            with sp.Fori(1, NS - 1) as S:
                superblock(S, False)
            for h in range(2):
                sp.dma_start(sa[:, h, :, :], adj_half[h, :, :, 0:P]).then_inc(ld_sa[h], 16)
            for i in range(2):
                sp.wait_ge(st_x1[i], ST0 + 16 * (NZP // 2))
            for k in range(4):
                sp.dma_start(xz[:, k, :], x1_d[k]).then_inc(ld_xz[k], 16)
            def reload(k):
                sp.wait_ge(zp_done, k - 3)
                sp.dma_start(xz[:, k % 4, :], x1_d[k]).then_inc(ld_xz[k % 4], 16)

            for k in range(4, 6):
                reload(k)
            load_x(NZP + 2, 0)
            store_x1(NZP, 0)
            for k in range(6, NZP):
                reload(k)
            load_x(NB - 1, 1)
            store_x1(NZP + 1, 1)
            store_x1(NZP + 2, 0)

            def load_half(i, h):
                sp.wait_ge(b_done, 2 * i + h - 1)
                sp.dma_start(sa[:, h, :, :], adj_half[h, :, :, bass.ts(i, P)]).then_inc(ld_sa[h], 16)

            load_half(1, 0)
            load_half(1, 1)
            store_x1(NB - 1, 1)
            with sp.Fori(2, H) as i:
                load_half(i, 0)
                load_half(i, 1)
            load_half(H, 0)
            load_half(H, 1)

            with sp.Fori(H + 1, NB) as i:
                load_half(i, 0)
                load_half(i, 1)
            for i in range(2):
                sp.wait_ge(st_x1[i], ST0 + 16 * (NB // 2))
                sp.dma_start(xe[:, i, :], x1_d[i]).then_inc(ld_xe[i], 16)
            sp.wait_ge(out_ready, N4)
            sp.wait_ge(st_u, 16 * (H - 1))
            for k in range(H - 1):
                sp.dma_start(z[:, H + k, :, :], u_d[k]).then_inc(ld_u[k], 16)
            sp.wait_ge(st_u, 16 * H)
            sp.dma_start(z[:, NB - 1, :, :], u_d[H - 1]).then_inc(ld_u[H - 1], 16)

            def final(m, b, i, more):
                sp.wait_ge(ln_out, LN0 + m + 1)
                sp.dma_start(out_blk[b], x1t[:, i, :]).then_inc(st_x1[i], 16)
                if more:
                    sp.wait_ge(out_free, N4 + b + 1)
                    sp.dma_start(xe[:, i, :], x1_d[b + 2]).then_inc(ld_xe[i], 16)

            with sp.Fori(0, NB // 2 - 1) as g:
                for i in range(2):
                    final(NB + 2 * g + i, 2 * g + i, i, True)
            for i in range(2):
                final(2 * NB - 2 + i, NB - 2 + i, i, False)
            for i in range(2):
                sp.wait_ge(st_x1[i], ST0 + 16 * NB)

        @block.gpsimd
        def _(pool):
            nc.gpsimd.memset(par[:, :], 0.0).then_inc(par_zero, 1)
            nc.gpsimd.memset(ident[:, :], 0.0).then_inc(ident_zero, 1)
            nc.gpsimd.memset(cst[:, 0:1], EPS).then_inc(consts, 1)
            nc.gpsimd.memset(cst[:, 1:2], 0.0).then_inc(consts, 1)
            nc.gpsimd.memset(nhalf[:, :], -0.5).then_inc(consts, 1)
            nc.gpsimd.memset(mv[:, :, :], 0.0).then_inc(ln_out, LN0)
            nc.gpsimd.memset(colsum[:, :, :], 0.0).then_inc(at_done, AT0)
            nc.gpsimd.memset(rowsum[:, :], 0.0).then_inc(rs_done, RS0)
            for i in range(2):
                nc.gpsimd.memset(rv[:, i, :], 0.0).then_inc(st_x1[i], ST0)
            pool.wait_ge(ident_zero, 1)
            nc.gpsimd.affine_select(out=ident[:, :], in_=ident[:, :], compare_op=ALU.not_equal, fill=1.0,
                                    base=0, pattern=[[-1, P]], channel_multiplier=1).then_inc(ident_done, 1)
            pool.wait_ge(ld_par, 64)
            nc.gpsimd.partition_all_reduce(parb[:, :], par[:, :], P, RADD).then_inc(par_all, 1)
            pool.wait_ge(w_mom, 1)
            nc.gpsimd.partition_all_reduce(wst[:, 3:4], wst[:, 0:1], P, RADD).then_inc(w_tot, 1)
            pool.wait_ge(w_step, 3)
            nc.gpsimd.partition_all_reduce(wst[:, 4:5], wst[:, 2:3], P, RADD).then_inc(w_tot, 1)
            pool.wait_ge(w_step, 4)
            pool.wait_ge(consts, 3)
            nc.gpsimd.tensor_tensor(wst[:, 6:7], wst[:, 5:6], nhalf[:, 0:1], ALU.pow).then_inc(w_tot, 1)

            def levels(b):
                pool.wait_ge(x_clip, b + 1)
                nc.gpsimd.tensor_scalar(xr[:, b, :], xr[:, b, :], BITS_A, MAGIC, ALU.mult, ALU.add).then_inc(x_int, 1)

            for b in range(H):
                levels(b)

            def largest(S):
                pool.wait_ge(rmx_part, S + 1)
                nc.gpsimd.tensor_tensor(rmx[:, 2:3], rmx[:, 0:1], cst[:, 1:2], ALU.add).then_inc(rmx_copy, 1)
                pool.wait_ge(consts, 3)
                pool.wait_ge(rmx_copy, S + 1)
                nc.gpsimd.partition_all_reduce(rmx[:, 1:2], rmx[:, 2:3], P, RMAX).then_inc(rmx_all, 1)

            for b in range(NB):
                pool.wait_ge(clip_done, b + 1)
                nc.gpsimd.tensor_scalar(q_sb[:, b, :], t1[:, b % 2, :], 1.0, -MAGIC, ALU.mult, ALU.add).then_inc(q_done, 1)
                if b == 2 * (G0 + J - 1):
                    largest(0)
                if b + H < NB:
                    levels(b + H)

            def rstd(m, i):
                pool.wait_ge(mv_done, m + 1)
                nc.gpsimd.tensor_tensor(rv[:, i, 0:1], mv[:, i, 1:2], cst[:, 0:1], ALU.add).then_inc(ve_done, 1)
                pool.wait_ge(ve_done, m + 1)
                nc.gpsimd.tensor_tensor(rv[:, i, 1:2], rv[:, i, 0:1], nhalf[:, 0:1], ALU.pow).then_inc(rstd_done, 1)
                pool.wait_ge(consts, 3)
                pool.wait_ge(rstd_done, m + 1)
                nc.gpsimd.tensor_scalar(rv[:, i, 2:3], mv[:, i, 0:1], rv[:, i, 1:2], -1.0,
                                        ALU.mult, ALU.mult).then_inc(nmr_done, 1)

            with pool.Fori(0, NS - 1) as S:
                for j in range(J - 1):
                    rstd(S * J + j, j % 2)
                largest(S + 1)
                rstd(S * J + J - 1, (J - 1) % 2)
            pool.wait_ge(dg_step, NS + 6)
            nc.gpsimd.tensor_tensor(dpow[:, :], degm[:, :], nhalf[:, :], ALU.pow).then_inc(dg_pow, 1)
            for j in range(J):
                rstd(NZP + j, j % 2)
            with pool.Fori(H, NB) as i:
                pool.wait_ge(out_free, N3 + i + 1)
                pool.dma_start(u_d[i - H], u_st).then_inc(st_u, 16)
            with pool.Fori(0, NB // 2) as g:
                for i in range(2):
                    rstd(NB + 2 * g + i, i)

        @block.scalar
        def _(act):
            def x_hi(b, i):
                act.wait_ge(xt_done, b + 1)
                if not isinstance(b, int) or b >= 2:
                    act.wait_ge(out_ready, b - 1)
                nc.scalar.activation(xit[:, i, 0, :], ps[:, XT + i, :], ACT.Copy, bias=-MAGIC).then_inc(xh_done, 1)

            def relu(b, i):
                act.wait_ge(out_ready, b + 1)
                if not isinstance(b, int) or b >= 2:
                    act.wait_ge(q_done, b - 1)
                else:
                    act.wait_ge(par_step, 4)
                nc.scalar.activation(t1[:, i, :], ps[:, OUT + i, :], ACT.Relu, scale=c1[:, 0:1]).then_inc(out_free, 1)

            x_hi(0, 0)
            x_hi(1, 1)
            relu(0, 0)
            with act.Fori(1, NB // 2) as g:
                x_hi(2 * g, 0)
                relu(2 * g - 1, 1)
                x_hi(2 * g + 1, 1)
                relu(2 * g, 0)
            relu(NB - 1, 1)

            def at_high(S, k):
                act.wait_ge(tb_ready, S * NB + k + 1)
                nc.scalar.activation(at_hi[:, k, bass.ts(S, J * P)], ps[:, TB + k % 4, :], ACT.Copy,
                                     scale=s_a[:, bass.ds(S, 1)],
                                     accum_out=colsum[:, k, bass.ds(S, 1)]).then_inc(ah_done, 1)

            def sum_rows(S, j):
                act.wait_ge(ld_nat[j], 16 * S + 16)
                act.wait_ge(rs_done, RS0 + S * J + j)
                nc.scalar.activation(dump[:, :], nat[:, j, :], ACT.Copy,
                                     accum_out=rowsum[:, bass.ds(S * J + j, 1)]).then_inc(rs_done, 1)

            def normalise(m, i, used):
                act.wait_ge(nmr_done, m + 1)
                act.wait_ge(st_x1[i], used)
                nc.scalar.activation(x1t[:, i, :], ts[:, i, :], ACT.Identity, scale=rv[:, i, 1:2],
                                     bias=rv[:, i, 2:3]).then_inc(ln_out, 1)

            def split_adj(S, first):
                act.wait_ge(sc_done, S + 1)
                for k in range(NB):
                    at_high(S, k)
                    if k == 3 * NB // 4 - 1 and not first:
                        normalise(S * J - 1, (J - 1) % 2, ST0 + 32 * S - 16)

            def superblock(S, first):
                split_adj(S, first)
                if first:
                    sum_rows(S, 0)
                    sum_rows(S, 1)
                at = 0
                for j, rows in ((0, 1), (1, 2), (2, 1)):
                    normalise(S * J + j, j % 2, ST0 + 32 * S + 16 * (j // 2))
                    if first and j == 0:
                        sum_rows(S, 2)
                        sum_rows(S, 3)
                    for jj in range(at, at + rows):
                        sum_rows(S + 1, jj)
                    at += rows

            superblock(0, True)
            with act.Fori(1, NS - 1) as S:
                superblock(S, False)
            split_adj(NS - 1, False)

            def z_back(k):
                act.wait_ge(ld_xz[k % 4], 16 * (k // 4) + 16)
                nc.scalar.activation(z[:, k, 0, :], xz[:, k % 4, :], ACT.Copy, scale=dz[:, k:k + 1]).then_inc(zph, 1)

            def z_here(j):
                k = NZP + j
                act.wait_ge(ln_out, LN0 + k + 1)
                nc.scalar.activation(z[:, k, 0, :], x1t[:, j % 2, :], ACT.Copy, scale=dz[:, k:k + 1]).then_inc(zdh, 1)

            def last_norm(j):
                if j >= 2:
                    act.wait_ge(zd_done, j - 1)
                normalise(NZP + j, j % 2, ST0 + 16 * ((NZP + j) // 2))

            def b_high(i, h, diagonal):
                if diagonal:
                    act.wait_ge(diag, i + 1)
                else:
                    act.wait_ge(add2, 2 * i + h + 1)
                if not isinstance(i, int) or i > 0:
                    if h == 0:
                        act.wait_ge(half_used, i)
                    else:
                        act.wait_ge(out_ready, N3 + i)
                nc.scalar.activation(bb[:, h, 0, :, :], sa[:, h, :, :], ACT.Copy, scale=bsc[:, 2:3]).then_inc(bh_done, 1)

            def u_high(i, dst):
                act.wait_ge(out_ready, N3 + i + 1)
                nc.scalar.activation(dst, bank(i), ACT.Copy, scale=eu[:, bass.ds(i, 1)]).then_inc(uh_done, 1)

            def u_staged(i):
                act.wait_ge(st_u, 16 * (i - H))
                u_high(i, u_st[:, 0, :])

            act.wait_ge(dg_done, 1)
            act.wait_ge(at_done, AT0 + NS * NB)
            for k in range(0, 4):
                z_back(k)
            last_norm(0)
            for k in range(4, 8):
                z_back(k)
            last_norm(1)
            for k in range(8, NZP):
                z_back(k)
            z_here(0)
            z_here(1)
            act.wait_ge(zp_done, NZP)
            b_high(0, 0, True)
            b_high(0, 1, False)
            last_norm(2)
            z_here(2)
            last_norm(3)
            z_here(3)
            with act.Fori(1, H) as i:
                b_high(i, 0, True)
                u_high(i - 1, q_u[:, bass.ds(i - 1, 1), 0, :].rearrange("p a f -> p (a f)"))
                b_high(i, 1, False)
            b_high(H, 0, False)
            u_high(H - 1, q_u[:, H - 1, 0, :])
            b_high(H, 1, True)
            act.wait_ge(zd_done, J)
            act.wait_ge(st_x1[0], ST0 + 16 * (NB // 2))
            b_high(H + 1, 0, False)
            u_high(H, u_st[:, 0, :])
            b_high(H + 1, 1, True)
            with act.Fori(H + 2, NB) as i:
                b_high(i, 0, False)
                u_staged(i - 1)
                b_high(i, 1, True)
            u_staged(NB - 1)
            act.wait_ge(st_u, 16 * H)
            with act.Fori(0, NB // 2) as g:
                for i in range(2):
                    normalise(NB + 2 * g + i, i, ST0 + 16 * (NB // 2) + 16 * g)

        @block.vector
        def _(dve):
            def step(s, n, ins):
                ins.then_inc(s, 1)
                dve.wait_ge(s, n)

            for c in range(FC):
                dve.wait_ge(ld_w[c], 16)
                nc.vector.bn_stats(wbn[:, c, :], wr[:, c, :]).then_inc(w_stat, 1)
            dve.wait_ge(w_stat, FC)
            nc.vector.bn_aggr(wst[:, 0:2], wbn[:, :, :].rearrange("p c s -> p (c s)")).then_inc(w_mom, 1)
            dve.wait_ge(par_all, 1)
            step(par_step, 1, nc.vector.reciprocal(pinv[:, :], parb[:, :]))
            dve.wait_ge(w_tot, 1)
            step(w_step, 1, nc.vector.tensor_scalar(wst[:, 3:4], wst[:, 3:4], -1.0 / P, None, ALU.mult))
            step(w_step, 2, nc.vector.tensor_scalar(wst[:, 2:3], wst[:, 0:1], wst[:, 3:4], None, ALU.add))
            nc.vector.scalar_tensor_tensor(out=wst[:, 2:3], in0=wst[:, 2:3], scalar=wst[:, 2:3],
                                           in1=wst[:, 1:2], op0=ALU.mult, op1=ALU.add).then_inc(w_step, 1)

            def clip_x(b, blocks):
                if b % 4 == 0:
                    dve.wait_ge(ld_x[b // 4], 16)
                v = xr[:, b:b + blocks, :]
                nc.vector.tensor_scalar(v, v, pinv[:, ALPHA_A:ALPHA_A + 1], 1.0, ALU.mult,
                                        ALU.min).then_inc(x_clip, blocks)

            dve.wait_ge(w_tot, 2)
            nc.vector.tensor_scalar(wst[:, 5:6], wst[:, 4:5], WN / (WN - 1.0) / P, None, ALU.mult).then_inc(w_step, 1)
            clip_x(0, 1)
            clip_x(1, 1)
            dve.wait_ge(w_tot, 3)
            step(w_step, 5, nc.vector.tensor_scalar(wst[:, 7:8], wst[:, 6:7], pinv[:, ALPHA_W:ALPHA_W + 1], BITS_W,
                                                    ALU.mult, ALU.mult))
            step(w_step, 6, nc.vector.tensor_scalar(wr, wr, wst[:, 3:4], wst[:, 7:8], ALU.add, ALU.mult))
            step(w_step, 7, nc.vector.tensor_scalar(wr, wr, BITS_W, -BITS_W, ALU.min, ALU.max))
            nc.vector.tensor_scalar(wi[:, :, :], wr, MAGIC, -MAGIC, ALU.add, ALU.add).then_inc(wi_done, 1)
            nc.vector.tensor_scalar(c1[:, :], parb[:, ALPHA_A:ALPHA_A + 1], 1.0 / BITS_A,
                                    parb[:, ALPHA_W:ALPHA_W + 1], ALU.mult, ALU.mult).then_inc(par_step, 1)
            nc.vector.tensor_scalar(k2[:, :], parb[:, ALPHA_A2:ALPHA_A2 + 1], 1.0 / BITS_A,
                                    parb[:, SF:SF + 1], ALU.mult, ALU.mult).then_inc(par_step, 1)
            dve.wait_ge(par_step, 3)
            nc.vector.tensor_scalar(c1[:, :], c1[:, :], pinv[:, ALPHA_A2:ALPHA_A2 + 1], BITS_A / BITS_W,
                                    ALU.mult, ALU.mult).then_inc(par_step, 1)
            nc.vector.tensor_scalar(k2[:, :], k2[:, :], pinv[:, SF:SF + 1], None, ALU.mult).then_inc(par_step, 1)
            clip_x(2, 1)
            clip_x(3, 1)

            def row_max(S, j):
                dve.wait_ge(ld_nat[j], 16 * S + 16)
                nc.vector.tensor_reduce(rmax[:, 2 * j:2 * j + 2],
                                        nat[:, j, :].rearrange("p (h n) -> p h n", h=2), AX.X, ALU.max,
                                        apply_absolute_value=True).then_inc(rmax_done, 1)

            def scales(S):
                def col(t):
                    return t[:, bass.ds(S, 1)]
                dve.wait_ge(rmax_done, J * S + J)
                nc.vector.tensor_reduce(rmx[:, 0:1], rmax[:, :], AX.X, ALU.max).then_inc(rmx_part, 1)
                dve.wait_ge(rmx_all, S + 1)
                step(sc_step, 2 * S + 1, nc.vector.tensor_scalar(
                    col(pow2).bitcast(I32), rmx[:, 1:2].bitcast(I32), EXPONENT, None, ALU.bitwise_and))
                step(sc_step, 2 * S + 2, nc.vector.tensor_scalar(
                    col(inv_a), col(pow2), 2.0 ** -100, 1.0 / TOP, ALU.max, ALU.mult))
                nc.vector.reciprocal(col(s_a), col(inv_a))
                nc.vector.tensor_scalar(col(c2), col(inv_a), k2[:, 0:1], None, ALU.mult)
                nc.vector.tensor_scalar(col(c4), col(inv_a), 1.0 / US, None, ALU.mult).then_inc(sc_done, 1)

            def x_lo(b, i):
                dve.wait_ge(xh_done, b + 1)
                nc.vector.scalar_tensor_tensor(out=xit[:, i, 1, :], in0=ps[:, XT + i, :], scalar=-MAGIC,
                                               in1=xit[:, i, 0, :].bitcast(F32), op0=ALU.add,
                                               op1=ALU.subtract).then_inc(xl_done, 1)

            def clip(b, i):
                dve.wait_ge(out_free, b + 1)
                nc.vector.tensor_scalar(t1[:, i, :], t1[:, i, :], BITS_A, MAGIC, ALU.min, ALU.add).then_inc(clip_done, 1)

            x_lo(0, 0)
            x_lo(1, 1)
            clip_x(4, 4)
            clip(0, 0)

            def pair(g, rows):
                for i in range(2):
                    x_lo(2 * g + i, i)
                    clip(2 * g + i - 1, 1 - i)
                    if rows:
                        n = N // 2
                        part = nat[:, bass.ds(g - G0, 1), i * n:(i + 1) * n].rearrange("p a n -> p (a n)")
                        ins = nc.vector.tensor_reduce(rmax[:, bass.ds(2 * (g - G0) + i, 1)], part, AX.X, ALU.max,
                                                      apply_absolute_value=True)
                        if i == 1:
                            ins.then_inc(rmax_done, 1)

            pair(1, False)
            clip_x(8, 4)
            pair(2, False)
            clip_x(12, 4)
            for j in range(J):
                dve.wait_ge(ld_nat[j], 16)
            with dve.Fori(G0, G0 + J) as g:
                pair(g, True)
            scales(0)
            with dve.Fori(G0 + J, NB // 2) as g:
                pair(g, False)
            clip(NB - 1, 1)

            def at_low(S, k):
                dve.wait_ge(ah_done, S * NB + k + 1)
                nc.vector.scalar_tensor_tensor(out=at_lo[:, k, bass.ts(S, J * P)], in0=ps[:, TB + k % 4, :],
                                               scalar=s_a[:, bass.ds(S, 1)], in1=at_hi[:, k, bass.ts(S, J * P)],
                                               op0=ALU.mult, op1=ALU.subtract).then_inc(at_done, 1)

            def residual(m, n, i, scale):
                dve.wait_ge(out_ready, n + 1)
                dve.wait_ge(ld_xe[i], 16 * (m // 2) + 16)
                dve.wait_ge(ln_out, LN0 + m - 1)
                nc.vector.scalar_tensor_tensor(out=ts[:, i, :], in0=ps[:, OUT + i, :], scalar=scale,
                                               in1=xe[:, i, :], op0=ALU.mult, op1=ALU.add).then_inc(out_free, 1)

            def moments(m, n, i, scale):
                residual(m, n, i, scale)
                statistics(m, n, i)

            def statistics(m, n, i):
                dve.wait_ge(out_free, n + 1)
                nc.vector.bn_stats(bst[:, :], ts[:, i, :]).then_inc(bs_done, 1)
                dve.wait_ge(consts, 3)
                dve.wait_ge(bs_done, m + 1)
                nc.vector.bn_aggr(mv[:, i, :], bst[:, :]).then_inc(mv_done, 1)

            def split_adj(S, first):
                for k in range(NB):
                    at_low(S, k)
                    m, n, i = S * J - 1, N2 + S * J - 1, (J - 1) % 2
                    if k == 3 and not first:
                        residual(m, n, i, c2[:, bass.ds(S - 1, 1)])
                    if k == 7 and not first:
                        statistics(m, n, i)

            def superblock(S, first):
                split_adj(S, first)
                at = 0
                for j, rows in ((0, 1), (1, 2), (2, 1)):
                    moments(S * J + j, N2 + S * J + j, j % 2, c2[:, bass.ds(S, 1)])
                    for jj in range(at, at + rows):
                        row_max(S + 1, jj)
                    at += rows
                scales(S + 1)

            superblock(0, True)
            with dve.Fori(1, NS - 1) as S:
                superblock(S, False)
            split_adj(NS - 1, False)

            step(dg_step, 1, nc.vector.tensor_reduce(bsc[:, 0:1], pow2[:, :], AX.X, ALU.max))
            step(dg_step, 2, nc.vector.tensor_scalar(bsc[:, 0:1], bsc[:, 0:1], 4.0, 2.0, ALU.mult, ALU.add))
            step(dg_step, 3, nc.vector.tensor_scalar(bsc[:, 3:4].bitcast(I32), bsc[:, 0:1].bitcast(I32),
                                                     EXPONENT, None, ALU.bitwise_and))
            step(dg_step, 4, nc.vector.tensor_scalar(bsc[:, 1:2], bsc[:, 3:4], 1.0 / TOP, None, ALU.mult))
            nc.vector.reciprocal(bsc[:, 2:3], bsc[:, 1:2])
            for S in range(NS):
                if S == 0:
                    dve.wait_ge(rs_done, RS0 + NB)
                nc_in1 = rowsum[:, :] if S == 0 else deg[:, :]
                step(dg_step, 5 + S, nc.vector.scalar_tensor_tensor(
                    out=deg[:, :], in0=colsum[:, :, S], scalar=inv_a[:, S:S + 1], in1=nc_in1,
                    op0=ALU.mult, op1=ALU.add))
            step(dg_step, 9, nc.vector.tensor_scalar(deg[:, :], deg[:, :], 0.5, 1.0, ALU.mult, ALU.add))
            nc.vector.tensor_scalar(degm[:, :], deg[:, :], 1e-30, None, ALU.max).then_inc(dg_step, 1)
            dve.wait_ge(dg_pow, 1)
            step(dg_step, 11, nc.vector.scalar_tensor_tensor(out=dinv[:, :], in0=deg[:, :], scalar=0.0,
                                                             in1=dpow[:, :], op0=ALU.is_gt, op1=ALU.mult))
            nc.vector.tensor_scalar(eu[:, :], dinv[:, :], bsc[:, 1:2], 0.5 * US / ZS, ALU.mult, ALU.mult)
            step(dg_done, 1, nc.vector.tensor_scalar(dz[:, :], dinv[:, :], ZS, None, ALU.mult))

            def z_back(k):
                dve.wait_ge(zph, k + 1)
                nc.vector.scalar_tensor_tensor(out=z[:, k, 1, :], in0=xz[:, k % 4, :], scalar=dz[:, k:k + 1],
                                               in1=z[:, k, 0, :], op0=ALU.mult, op1=ALU.subtract).then_inc(zp_done, 1)

            def z_here(j):
                k = NZP + j
                dve.wait_ge(zdh, j + 1)
                nc.vector.scalar_tensor_tensor(out=z[:, k, 1, :], in0=x1t[:, j % 2, :], scalar=dz[:, k:k + 1],
                                               in1=z[:, k, 0, :], op0=ALU.mult, op1=ALU.subtract).then_inc(zd_done, 1)

            def add_half(i, h, diagonal):
                n = 2 * i + h
                S = i // J
                inv = inv_a[:, bass.ds(S, 1)]
                dve.wait_ge(ld_sa[h], 16 * i + 16)
                nc.vector.scalar_tensor_tensor(out=sa[:, h, :, :], in0=at_hi[:, H * h:H * h + H, bass.ts(i, P)],
                                               scalar=inv, in1=sa[:, h, :, :], op0=ALU.mult,
                                               op1=ALU.add).then_inc(add1, 1)
                dve.wait_ge(add1, n + 1)
                nc.vector.scalar_tensor_tensor(out=sa[:, h, :, :], in0=at_lo[:, H * h:H * h + H, bass.ts(i, P)],
                                               scalar=inv, in1=sa[:, h, :, :], op0=ALU.mult,
                                               op1=ALU.add).then_inc(add2, 1)
                if diagonal:
                    dve.wait_ge(add2, n + 1)
                    d = sa[:, h, bass.ds(i - H * h, 1), :].rearrange("p a c -> p (a c)")
                    nc.vector.scalar_tensor_tensor(out=d, in0=ident[:, :], scalar=2.0, in1=d, op0=ALU.mult,
                                                   op1=ALU.add).then_inc(diag, 1)

            def b_low(i, h):
                dve.wait_ge(bh_done, 2 * i + h + 1)
                nc.vector.scalar_tensor_tensor(out=bb[:, h, 1, :, :], in0=sa[:, h, :, :], scalar=bsc[:, 2:3],
                                               in1=bb[:, h, 0, :, :], op0=ALU.mult,
                                               op1=ALU.subtract).then_inc(b_done, 1)

            def u_low(i, hi, lo):
                dve.wait_ge(uh_done, i + 1)
                nc.vector.scalar_tensor_tensor(out=lo, in0=bank(i), scalar=eu[:, bass.ds(i, 1)], in1=hi,
                                               op0=ALU.mult, op1=ALU.subtract).then_inc(out_free, 1)

            def last_moments(j):
                moments(NZP + j, N2 + NZP + j, j % 2, c2[:, NS - 1:NS])

            for k in range(0, 4):
                z_back(k)
            last_moments(0)
            for k in range(4, 8):
                z_back(k)
            last_moments(1)
            for k in range(8, NZP):
                z_back(k)
            z_here(0)
            z_here(1)
            add_half(0, 0, True)
            add_half(0, 1, False)
            b_low(0, 0)
            last_moments(2)
            b_low(0, 1)
            z_here(2)
            last_moments(3)
            z_here(3)

            def strip(i, first, hi, lo):
                add_half(i, 0, first)
                b_low(i, 0)
                add_half(i, 1, not first)
                u_low(i - 1, hi, lo)
                b_low(i, 1)

            def u_block(i, t):
                return q_u[:, bass.ds(i, 1), t, :].rearrange("p a f -> p (a f)")

            with dve.Fori(1, H) as i:
                strip(i, True, u_block(i - 1, 0), u_block(i - 1, 1))
            strip(H, False, q_u[:, H - 1, 0, :], q_u[:, H - 1, 1, :])
            with dve.Fori(H + 1, NB) as i:
                strip(i, False, u_st[:, 0, :], u_st[:, 1, :])
            u_low(NB - 1, u_st[:, 0, :], u_st[:, 1, :])
            with dve.Fori(0, NS) as S:
                for j in range(J):
                    moments(NB + S * J + j, N4 + S * J + j, j % 2, c4[:, bass.ds(S, 1)])

        @block.tensor
        def _(pe):
            pe.wait_ge(ident_done, 1)

            def turn_x(b):
                pe.wait_ge(x_int, b + 1)
                if b >= 2:
                    pe.wait_ge(xl_done, b - 1)
                for c in range(FC):
                    mm = nc.tensor.transpose(ps[:, XT + b % 2, c * P:(c + 1) * P], xr[:, b, c * P:(c + 1) * P],
                                             ident[:, :])
                mm.then_inc(xt_done, 1)

            def times_w(b):
                pe.wait_ge(xl_done, b + 1)
                if b == 0:
                    pe.wait_ge(wi_done, 1)
                if b >= 2:
                    pe.wait_ge(out_free, b - 1)
                for c in range(FC):
                    for t in range(2):
                        mm = nc.tensor.matmul(ps[:, OUT + b % 2, :], xit[:, b % 2, t, c * P:(c + 1) * P],
                                              wi[:, c, :], start=(c + t == 0), stop=(c == FC - 1 and t == 1))
                mm.then_inc(out_ready, 1)

            def turn_adj(S, k):
                pe.wait_ge(at_done, S * NB + k + 1)
                for j in range(J):
                    if k == 0:
                        pe.wait_ge(ld_nat[j], 16 * S + 16)
                    mm = nc.tensor.transpose(ps[:, TB + k % 4, j * P:(j + 1) * P], nat[:, j, k * P:(k + 1) * P],
                                             ident[:, :])
                mm.then_inc(tb_ready, 1)

            turn_x(0)
            for b in range(NB):
                if b + 1 < NB:
                    turn_x(b + 1)
                else:
                    for k in range(LEAD):
                        turn_adj(0, k)
                times_w(b)

            def superblock(S, last):
                for j in range(J):
                    pe.wait_ge(out_free, N2 + S * J + j - 1)
                    for k in range(NB):
                        if j == 0:
                            if k + LEAD < NB:
                                turn_adj(S, k + LEAD)
                            pe.wait_ge(at_done, AT0 + S * NB + k + 1)
                            if k == 0:
                                pe.wait_ge(q_done, NB)
                        if j == J - 1 and k == NB - 4 and not last:
                            for kk in range(LEAD):
                                turn_adj(S + 1, kk)
                        for a in (at_hi, at_lo):
                            mm = nc.tensor.matmul(ps[:, OUT + j % 2, :], a[:, k, bass.ts(S * J + j, P)],
                                                  q_sb[:, k, :], start=(k == 0 and a is at_hi),
                                                  stop=(k == NB - 1 and a is at_lo))
                    mm.then_inc(out_ready, 1)

            with pe.Fori(0, NS - 1) as S:
                superblock(S, False)
            superblock(NS - 1, True)

            def times_z(i, parity, first):
                pe.wait_ge(out_free, N3 + i - 1)
                for h in range(2):
                    pe.wait_ge(b_done, 2 * i + h + 1)
                    for kk in range(H):
                        k = h * H + kk
                        if first and k >= NZP:
                            pe.wait_ge(zd_done, k - NZP + 1)
                        for a, t in ((0, 0), (0, 1), (1, 0)):
                            mm = nc.tensor.matmul(ps[:, OUT + parity, :], bb[:, h, a, kk, :], z[:, k, t, :],
                                                  start=(k == 0 and a + t == 0), stop=(k == NB - 1 and a == 1))
                    mm.then_inc(half_used if h == 0 else out_ready, 1)

            times_z(0, 0, True)
            times_z(1, 1, False)
            with pe.Fori(1, NB // 2) as g:
                times_z(2 * g, 0, False)
                times_z(2 * g + 1, 1, False)

            def times_u(g, first):
                for i in range(2):
                    pe.wait_ge(out_free, N4 + 2 * g + i - 1)
                    for k in range(NB):
                        if first and i == 0:
                            if k < H:
                                pe.wait_ge(out_free, N3 + k + 1)
                            else:
                                pe.wait_ge(ld_u[k - H], 16)
                        u = q_u[:, k, :, :] if k < H else z[:, k, :, :]
                        for a, t in ((at_hi, 0), (at_hi, 1), (at_lo, 0)):
                            mm = nc.tensor.matmul(ps[:, OUT + i, :], a[:, k, bass.ts(2 * g + i, P)], u[:, t, :],
                                                  start=(k == 0 and a is at_hi and t == 0),
                                                  stop=(k == NB - 1 and a is at_lo))
                    mm.then_inc(out_ready, 1)

            times_u(0, True)
            with pe.Fori(1, NB // 2) as g:
                times_u(g, False)


_INS = ["x", "adj", "L0_gnn_adj_scaling_factor", "L0_gnn_weight", "L0_gnn_wgt_alpha", "L0_gnn_act_alpha",
        "L0_gnn_act_alpha2"]


def kernel(**inputs):
    import numpy as _np
    import concourse.bacc as _bacc
    from concourse import mybir as _mybir
    from concourse.bass_utils import run_bass_kernel_spmd as _run

    nc = _bacc.Bacc("TRN2", target_bir_lowering=False, num_devices=1)
    arrays, args = {}, []
    for name in _INS:
        a = _np.ascontiguousarray(inputs[name])
        arrays[f"in_{name}_dram"] = a
        args.append(nc.dram_tensor(f"in_{name}_dram", a.shape, _mybir.dt.from_np(a.dtype), kind="ExternalInput").ap())
    args.append(nc.dram_tensor("out_0_dram", inputs["x"].shape, _mybir.dt.float32, kind="ExternalOutput").ap())
    build(nc, *args)
    r = _run(nc, [arrays], core_ids=[0])
    return r.results[0]["out_0_dram"]
```

```python
from contextlib import ExitStack

import concourse.bass as bass
from concourse import mybir

F32 = mybir.dt.float32
F32R = mybir.dt.float32r
F16 = mybir.dt.float16
U8 = mybir.dt.uint8
I32 = mybir.dt.int32
ALU = mybir.AluOpType
ACT = mybir.ActivationFunctionType
AX = mybir.AxisListType
RMAX = bass.bass_isa.ReduceOp.max
RADD = bass.bass_isa.ReduceOp.add

P = 128
MAGIC = 1.5 * 2.0 ** 23
EXPONENT = 0x7F800000
TOP = 2.0 ** 14
ZS = 2.0 ** 11
US = 2.0 ** 5
EPS = 1e-5
BITS_A = 15.0
BITS_W = 7.0
SF, ALPHA_W, ALPHA_A, ALPHA_A2 = range(4)


def build(nc, x, adj, sf, weight, wgt_alpha, act_alpha, act_alpha2, out):
    N, F = x.shape
    NB = N // P
    FC = F // P
    J = 4
    NS = NB // J
    LOADS = [(0, 2), (2, 2), (4, 4), (8, 4), (12, 4)]
    H = NB // 2
    NZP = NB - J
    AT0 = 4
    LEAD = 4
    G0 = 3
    LN0 = 2
    RS0 = 1
    ST0 = 16
    WARM = 45
    WN = F * F

    x_blk = x.rearrange("(b p) f -> b p f", p=P)
    x_rows = x.rearrange("(b p) f -> p b f", p=P)
    adj_rows = adj.rearrange("(b p) c -> b p c", p=P)
    adj_half = adj.rearrange("(h k p) c -> h p k c", p=P, h=2)
    w_v = weight.rearrange("(c p) n -> p c n", p=P)
    out_blk = out.rearrange("(b p) f -> b p f", p=P)
    x1_d = nc.dram_tensor("x1_scratch", (NB, P, F), F32, kind="Internal").ap()
    u_d = nc.dram_tensor("u_scratch", (H, P, 2, F), F16, kind="Internal").ap()

    with ExitStack() as ctx:
        def sb(name, shape, dt):
            return ctx.enter_context(nc.sbuf_tensor(name, shape, dt))

        def sem(name):
            return ctx.enter_context(nc.semaphore(name))

        at_hi = sb("at_hi", [P, NB, N], F16)
        at_lo = sb("at_lo", [P, NB, N], F16)
        q_u = sb("q_u", [P, H, 2, F], F16)
        q_sb = q_u[:, :, :, :].rearrange("p k t f -> p (k t) f")
        nat = sb("nat", [P, J, N], F32)
        z = nat[:, :, :].rearrange("p j n -> p (j n)").bitcast(F16).rearrange(
            "p (k t f) -> p k t f", k=NB, t=2)
        xe = sb("xe", [P, 2, F], F32)
        ts = sb("ts", [P, 2, F], F32)
        x1t = sb("x1t", [P, 2, F], F32)
        u_st = x1t[:, 0, :].bitcast(F16).rearrange("p (t f) -> p t f", t=2)
        dump = sb("dump", [P, N], U8)
        wbn = dump[:, 0:24 * FC].bitcast(F32).rearrange("p (c s) -> p c s", c=FC)
        ident = sb("ident", [P, P], F32)
        par = sb("par", [P, 4], F32)
        parb = sb("parb", [P, 4], F32)
        pinv = sb("pinv", [P, 4], F32)
        c1 = sb("c1", [P, 1], F32)
        k2 = sb("k2", [P, 1], F32)
        wst = sb("wst", [P, 8], F32)
        rmax = sb("rmax", [P, 2 * J], F32)
        rmx = sb("rmx", [P, 3], F32)
        cst = sb("cst", [P, 2], F32)
        pow2 = sb("pow2", [P, NS], F32)
        s_a = sb("s_a", [P, NS], F32)
        inv_a = sb("inv_a", [P, NS], F32)
        c2 = sb("c2", [P, NS], F32)
        c4 = sb("c4", [P, NS], F32)
        rowsum = sb("rowsum", [P, NB], F32)
        colsum = sb("colsum", [P, NB, NS], F32)
        deg = sb("deg", [P, NB], F32)
        degm = sb("degm", [P, NB], F32)
        dpow = sb("dpow", [P, NB], F32)
        dinv = sb("dinv", [P, NB], F32)
        dz = sb("dz", [P, NB], F32)
        eu = sb("eu", [P, NB], F32)
        nhalf = sb("nhalf", [P, NB], F32)
        bsc = sb("bsc", [P, 4], F32)
        bst = sb("bst", [P, 12], F32)
        mv = sb("mv", [P, 2, 2], F32)
        rv = sb("rv", [P, 2, 3], F32)

        with nc.sbuf_tensor("wi", [P, FC, F], F32R) as wi, nc.sbuf_tensor("xit", [P, 2, 2, F], F32R) as xit:
            pass
        sa = sb("sa", [P, 2, H, P], F32)
        bb = sb("bb", [P, 2, 2, H, P], F16)
        xz = bb[:, :, :, :, :].rearrange("p a t k c -> p (a t k c)").bitcast(F32).rearrange(
            "p (s f) -> p s f", s=4)
        xr = at_hi[:, :, N // 2:N].bitcast(F32)
        t1 = at_lo[:, 2:4, N // 2:N].bitcast(F32)
        wr = at_lo[:, 6:6 + FC, N // 2:N].bitcast(F32)

        ps = ctx.enter_context(nc.psum_tensor("ps", [P, 8, 512], F32))
        OUT, XT, TB = 0, 2, 4

        par_zero = sem("par_zero")
        ident_zero = sem("ident_zero")
        ident_done = sem("ident_done")
        consts = sem("consts")
        ld_par = sem("ld_par")
        ld_w = [sem(f"ld_w{c}") for c in range(FC)]
        ld_x = [sem(f"ld_x{g}") for g in range(len(LOADS))]
        ld_nat = [sem(f"ld_nat{j}") for j in range(J)]
        ld_xe = [sem(f"ld_xe{i}") for i in range(2)]
        ld_xz = [sem(f"ld_xz{i}") for i in range(4)]
        ld_sa = [sem(f"ld_sa{i}") for i in range(2)]
        ld_u = [sem(f"ld_u{i}") for i in range(H)]
        st_x1 = [sem(f"st_x1{i}") for i in range(2)]
        st_u = sem("st_u")
        par_all = sem("par_all")
        par_step = sem("par_step")
        w_step = sem("w_step")
        w_stat = sem("w_stat")
        w_mom = sem("w_mom")
        w_tot = sem("w_tot")
        w_mean = sem("w_mean")
        w_top = sem("w_top")
        w_level = sem("w_level")
        wi_done = sem("wi_done")
        x_clip = sem("x_clip")
        x_int = sem("x_int")
        xt_done = sem("xt_done")
        xh_done = sem("xh_done")
        xl_done = sem("xl_done")
        clip_done = sem("clip_done")
        q_done = sem("q_done")
        out_ready = sem("out_ready")
        out_free = sem("out_free")
        rmax_done = sem("rmax_done")
        rmx_part = sem("rmx_part")
        rmx_all = sem("rmx_all")
        rmx_copy = sem("rmx_copy")
        sc_step = sem("sc_step")
        sc_done = sem("sc_done")
        tb_ready = sem("tb_ready")
        ah_done = sem("ah_done")
        at_done = sem("at_done")
        rs_done = sem("rs_done")
        bs_done = sem("bs_done")
        mv_done = sem("mv_done")
        ve_done = sem("ve_done")
        rstd_done = sem("rstd_done")
        nmr_done = sem("nmr_done")
        ln_out = sem("ln_out")
        dg_step = sem("dg_step")
        dg_pow = sem("dg_pow")
        dg_done = sem("dg_done")
        zph = sem("zph")
        zp_done = sem("zp_done")
        zdh = sem("zdh")
        zd_done = sem("zd_done")
        add1 = sem("add1")
        add2 = sem("add2")
        diag = sem("diag")
        bh_done = sem("bh_done")
        b_done = sem("b_done")
        half_used = sem("half_used")
        uh_done = sem("uh_done")
        half_ready = sem("half_ready")
        half_sum = sem("half_sum")
        last_rstd = sem("last_rstd")
        last_out = sem("last_out")

        def bank(n):
            return ps[:, n % 2, :] if isinstance(n, int) else ps[:, bass.ds(n % 2, 1), :].rearrange("p a f -> p (a f)")

        N2, N3, N4 = NB, 2 * NB, 3 * NB
        block = ctx.enter_context(nc.Block())

        @block.sync
        def _(sp):
            for c in range(FC):
                sp.dma_start(wr[:, c, :], w_v[:, c, :]).then_inc(ld_w[c], 16)
            sp.wait_ge(par_zero, 1)
            for i, a in enumerate((sf, wgt_alpha, act_alpha, act_alpha2)):
                sp.dma_start(par[0:1, i:i + 1], a.rearrange("(a b) -> a b", a=1)).then_inc(ld_par, 16)
            for g, (b, n) in enumerate(LOADS):
                sp.dma_start(xr[:, b:b + n, :], x_rows[:, b:b + n, :]).then_inc(ld_x[g], 16)
            for j in range(J):
                sp.dma_start(nat[:, j, :], adj_rows[j]).then_inc(ld_nat[j], 16)
            for i in range(2):
                sp.dma_start(xe[:, i, :], x_blk[i]).then_inc(ld_xe[i], 16)

            def store_x1(m, i):
                sp.wait_ge(ln_out, LN0 + m + 1)
                sp.dma_start(x1_d[m], x1t[:, i, :]).then_inc(st_x1[i], 16)

            def load_x(m, i):
                sp.wait_ge(out_free, N2 + m - 1)
                sp.dma_start(xe[:, i, :], x_blk[m]).then_inc(ld_xe[i], 16)

            def superblock(S):
                sp.wait_ge(at_done, AT0 + S * NB + NB)
                for j in range(J):
                    sp.wait_ge(rs_done, RS0 + S * J + j + 1)
                    sp.dma_start(nat[:, j, :], adj_rows[S * J + J + j]).then_inc(ld_nat[j], 16)
                for j in range(J - 1):
                    load_x(S * J + j + 2, j % 2)
                    store_x1(S * J + j, j % 2)
                load_x(S * J + J + 1, 1)
                store_x1(S * J + J - 1, 1)

            sp.wait_ge(out_ready, NB)
            for h in range(2):
                sp.dma_start(sa[:, h, :, :], adj_half[h, :, :, 0:P]).then_inc(ld_sa[h], 16)
            with sp.Fori(0, NS - 1) as S:
                superblock(S)
            for i in range(2):
                sp.wait_ge(st_x1[i], ST0 + 16 * (NZP // 2))
            for k in range(4):
                sp.dma_start(xz[:, k, :], x1_d[k]).then_inc(ld_xz[k], 16)
            def reload(k):
                sp.wait_ge(zp_done, k - 3)
                sp.dma_start(xz[:, k % 4, :], x1_d[k]).then_inc(ld_xz[k % 4], 16)

            load_x(NZP + 2, 0)
            for k in range(4, 8):
                reload(k)
            store_x1(NZP, 0)
            load_x(NZP + 3, 1)
            for k in range(8, NZP):
                reload(k)
            store_x1(NZP + 1, 1)

            def load_half(i, h):
                sp.wait_ge(b_done, 2 * i + h - 1)
                sp.dma_start(sa[:, h, :, :], adj_half[h, :, :, bass.ts(i, P)]).then_inc(ld_sa[h], 16)

            load_half(1, 0)
            store_x1(NZP + 2, 0)
            load_half(1, 1)
            store_x1(NZP + 3, 1)
            with sp.Fori(2, H) as i:
                load_half(i, 0)
                load_half(i, 1)
            load_half(H, 0)
            load_half(H, 1)

            with sp.Fori(H + 1, NB) as i:
                load_half(i, 0)
                load_half(i, 1)
            for i in range(2):
                sp.wait_ge(st_x1[i], ST0 + 16 * (NB // 2))
                sp.dma_start(xe[:, i, :], x1_d[i]).then_inc(ld_xe[i], 16)
            sp.wait_ge(out_ready, N4)
            sp.wait_ge(st_u, 16 * (H - 1))
            for k in range(H - 1):
                sp.dma_start(z[:, H + k, :, :], u_d[k]).then_inc(ld_u[k], 16)
            sp.wait_ge(st_u, 16 * H)
            sp.dma_start(z[:, NB - 1, :, :], u_d[H - 1]).then_inc(ld_u[H - 1], 16)

            def final(m, b, i, more):
                sp.wait_ge(ln_out, LN0 + m + 1)
                sp.dma_start(out_blk[b], x1t[:, i, :]).then_inc(st_x1[i], 16)
                if more:
                    sp.wait_ge(out_free, N4 + b + 1)
                    sp.dma_start(xe[:, i, :], x1_d[b + 2]).then_inc(ld_xe[i], 16)

            with sp.Fori(0, NB // 2 - 1) as g:
                for i in range(2):
                    final(NB + 2 * g + i, 2 * g + i, i, True)
            final(2 * NB - 2, NB - 2, 0, False)
            sp.wait_ge(last_out, 1)
            sp.dma_start(out_blk[NB - 1], x1t[:, 1, :]).then_inc(st_x1[1], 16)
            for i in range(2):
                sp.wait_ge(st_x1[i], ST0 + 16 * NB)

        @block.gpsimd
        def _(pool):
            nc.gpsimd.memset(par[:, :], 0.0).then_inc(par_zero, 1)
            nc.gpsimd.memset(ident[:, :], 0.0).then_inc(ident_zero, 1)
            nc.gpsimd.memset(cst[:, 0:1], EPS).then_inc(consts, 1)
            nc.gpsimd.memset(cst[:, 1:2], 0.0).then_inc(consts, 1)
            nc.gpsimd.memset(nhalf[:, :], -0.5).then_inc(consts, 1)
            nc.gpsimd.memset(mv[:, :, :], 0.0).then_inc(ln_out, LN0)
            nc.gpsimd.memset(colsum[:, :, :], 0.0).then_inc(at_done, AT0)
            nc.gpsimd.memset(rowsum[:, :], 0.0).then_inc(rs_done, RS0)
            for i in range(2):
                nc.gpsimd.memset(rv[:, i, :], 0.0).then_inc(st_x1[i], ST0)
            pool.wait_ge(ident_zero, 1)
            nc.gpsimd.affine_select(out=ident[:, :], in_=ident[:, :], compare_op=ALU.not_equal, fill=1.0,
                                    base=0, pattern=[[-1, P]], channel_multiplier=1).then_inc(ident_done, 1)
            pool.wait_ge(ld_par, 64)
            nc.gpsimd.partition_all_reduce(parb[:, :], par[:, :], P, RADD).then_inc(par_all, 1)
            pool.wait_ge(w_mom, 1)
            nc.gpsimd.partition_all_reduce(wst[:, 3:4], wst[:, 0:1], P, RADD).then_inc(w_tot, 1)
            pool.wait_ge(w_step, 3)
            nc.gpsimd.partition_all_reduce(wst[:, 4:5], wst[:, 2:3], P, RADD).then_inc(w_tot, 1)
            pool.wait_ge(w_step, 4)
            pool.wait_ge(consts, 3)
            nc.gpsimd.tensor_tensor(wst[:, 6:7], wst[:, 5:6], nhalf[:, 0:1], ALU.pow).then_inc(w_tot, 1)

            def levels(b):
                pool.wait_ge(x_clip, b + 1)
                nc.gpsimd.tensor_scalar(xr[:, b, :], xr[:, b, :], BITS_A, MAGIC, ALU.mult, ALU.add).then_inc(x_int, 1)

            for b in range(H):
                levels(b)

            def largest(S):
                pool.wait_ge(rmx_part, S + 1)
                nc.gpsimd.tensor_tensor(rmx[:, 2:3], rmx[:, 0:1], cst[:, 1:2], ALU.add).then_inc(rmx_copy, 1)
                pool.wait_ge(consts, 3)
                pool.wait_ge(rmx_copy, S + 1)
                nc.gpsimd.partition_all_reduce(rmx[:, 1:2], rmx[:, 2:3], P, RMAX).then_inc(rmx_all, 1)

            for b in range(NB):
                pool.wait_ge(clip_done, b + 1)
                nc.gpsimd.tensor_scalar(q_sb[:, b, :], t1[:, b % 2, :], 1.0, -MAGIC, ALU.mult, ALU.add).then_inc(q_done, 1)
                if b == NB - 5:
                    largest(0)
                if b + H < NB:
                    levels(b + H)

            def rstd(m, i):
                pool.wait_ge(mv_done, m + 1)
                nc.gpsimd.tensor_tensor(rv[:, i, 0:1], mv[:, i, 1:2], cst[:, 0:1], ALU.add).then_inc(ve_done, 1)
                pool.wait_ge(ve_done, m + 1)
                nc.gpsimd.tensor_tensor(rv[:, i, 1:2], rv[:, i, 0:1], nhalf[:, 0:1], ALU.pow).then_inc(rstd_done, 1)
                pool.wait_ge(consts, 3)
                pool.wait_ge(rstd_done, m + 1)
                nc.gpsimd.tensor_scalar(rv[:, i, 2:3], mv[:, i, 0:1], rv[:, i, 1:2], -1.0,
                                        ALU.mult, ALU.mult).then_inc(nmr_done, 1)

            with pool.Fori(0, NS - 1) as S:
                for j in range(J - 1):
                    rstd(S * J + j, j % 2)
                largest(S + 1)
                rstd(S * J + J - 1, (J - 1) % 2)
            pool.wait_ge(dg_step, NS + 6)
            nc.gpsimd.tensor_tensor(dpow[:, :], degm[:, :], nhalf[:, :], ALU.pow).then_inc(dg_pow, 1)
            for j in range(J):
                rstd(NZP + j, j % 2)
            with pool.Fori(H, NB) as i:
                pool.wait_ge(out_free, N3 + i + 1)
                pool.dma_start(u_d[i - H], u_st).then_inc(st_u, 16)
            with pool.Fori(0, NB // 2 - 1) as g:
                for i in range(2):
                    rstd(NB + 2 * g + i, i)
            rstd(2 * NB - 2, 0)
            pool.wait_ge(mv_done, 2 * NB)
            nc.gpsimd.tensor_tensor(rv[:, 1, 0:1], mv[:, 1, 1:2], cst[:, 0:1], ALU.add).then_inc(ve_done, 1)
            pool.wait_ge(ve_done, 2 * NB)
            nc.gpsimd.tensor_tensor(rv[:, 1, 1:2], rv[:, 1, 0:1], nhalf[:, 0:1], ALU.pow).then_inc(last_rstd, 1)

        @block.scalar
        def _(act):
            def x_hi(b, i):
                act.wait_ge(xt_done, b + 1)
                if not isinstance(b, int) or b >= 2:
                    act.wait_ge(out_ready, b - 1)
                nc.scalar.activation(xit[:, i, 0, :], ps[:, XT + i, :], ACT.Copy, bias=-MAGIC).then_inc(xh_done, 1)

            def relu(b, i):
                act.wait_ge(out_ready, b + 1)
                if not isinstance(b, int) or b >= 2:
                    act.wait_ge(q_done, b - 1)
                else:
                    act.wait_ge(par_step, 4)
                nc.scalar.activation(t1[:, i, :], ps[:, OUT + i, :], ACT.Relu, scale=c1[:, 0:1]).then_inc(out_free, 1)

            def weight_int(c):
                act.wait_ge(w_level, c + 1)
                nc.scalar.activation(wi[:, c, :], wr[:, c, :], ACT.Copy, bias=-MAGIC).then_inc(wi_done, 1)

            act.wait_ge(w_step, 1)
            for c in range(FC):
                nc.scalar.activation(wr[:, c, :], wr[:, c, :], ACT.Identity, bias=wst[:, 3:4]).then_inc(w_mean, 1)
            x_hi(0, 0)
            weight_int(0)
            weight_int(1)
            x_hi(1, 1)
            weight_int(2)
            weight_int(3)
            x_hi(2, 0)
            relu(0, 0)
            x_hi(3, 1)
            relu(1, 1)
            with act.Fori(2, NB // 2) as g:
                for i in range(2):
                    x_hi(2 * g + i, i)
                    relu(2 * g + i - 2, i)
            relu(NB - 2, 0)

            def at_high(S, k):
                act.wait_ge(tb_ready, S * NB + k + 1)
                nc.scalar.activation(at_hi[:, k, bass.ts(S, J * P)], ps[:, TB + k % 4, :], ACT.Copy,
                                     scale=s_a[:, bass.ds(S, 1)],
                                     accum_out=colsum[:, k, bass.ds(S, 1)]).then_inc(ah_done, 1)

            def sum_rows(S, j):
                act.wait_ge(ld_nat[j], 16 * S + 16)
                act.wait_ge(rs_done, RS0 + S * J + j)
                nc.scalar.activation(dump[:, :], nat[:, j, :], ACT.Copy,
                                     accum_out=rowsum[:, bass.ds(S * J + j, 1)]).then_inc(rs_done, 1)

            def normalise(m, i, used):
                act.wait_ge(nmr_done, m + 1)
                act.wait_ge(st_x1[i], used)
                nc.scalar.activation(x1t[:, i, :], ts[:, i, :], ACT.Identity, scale=rv[:, i, 1:2],
                                     bias=rv[:, i, 2:3]).then_inc(ln_out, 1)

            def split_adj(S, first):
                act.wait_ge(sc_done, S + 1)
                for k in range(NB):
                    at_high(S, k)
                    if k == LEAD - 1 and first:
                        relu(NB - 1, 1)
                    if k == 3 * NB // 4 - 1 and not first:
                        normalise(S * J - 1, (J - 1) % 2, ST0 + 32 * S - 16)

            def superblock(S, first):
                split_adj(S, first)
                if first:
                    sum_rows(S, 0)
                    sum_rows(S, 1)
                at = 0
                for j, rows in ((0, 1), (1, 2), (2, 1)):
                    normalise(S * J + j, j % 2, ST0 + 32 * S + 16 * (j // 2))
                    if first and j == 0:
                        sum_rows(S, 2)
                        sum_rows(S, 3)
                    for jj in range(at, at + rows):
                        sum_rows(S + 1, jj)
                    at += rows

            superblock(0, True)
            with act.Fori(1, NS - 1) as S:
                superblock(S, False)
            split_adj(NS - 1, False)

            def z_back(k):
                act.wait_ge(ld_xz[k % 4], 16 * (k // 4) + 16)
                nc.scalar.activation(z[:, k, 0, :], xz[:, k % 4, :], ACT.Copy, scale=dz[:, k:k + 1]).then_inc(zph, 1)

            def z_here(j):
                k = NZP + j
                act.wait_ge(ln_out, LN0 + k + 1)
                nc.scalar.activation(z[:, k, 0, :], x1t[:, j % 2, :], ACT.Copy, scale=dz[:, k:k + 1]).then_inc(zdh, 1)

            def last_norm(j):
                if j >= 2:
                    act.wait_ge(zd_done, j - 1)
                normalise(NZP + j, j % 2, ST0 + 16 * ((NZP + j) // 2))

            def b_high(i, h, diagonal):
                if diagonal:
                    act.wait_ge(diag, i + 1)
                else:
                    act.wait_ge(add2, 2 * i + h + 1)
                if not isinstance(i, int) or i > 0:
                    if h == 0:
                        act.wait_ge(half_used, i)
                    else:
                        act.wait_ge(out_ready, N3 + i)
                nc.scalar.activation(bb[:, h, 0, :, :], sa[:, h, :, :], ACT.Copy, scale=bsc[:, 2:3]).then_inc(bh_done, 1)

            def u_high(i, dst):
                act.wait_ge(out_ready, N3 + i + 1)
                nc.scalar.activation(dst, bank(i), ACT.Copy, scale=eu[:, bass.ds(i, 1)]).then_inc(uh_done, 1)

            def u_staged(i):
                act.wait_ge(st_u, 16 * (i - H))
                u_high(i, u_st[:, 0, :])

            act.wait_ge(dg_done, 1)
            act.wait_ge(at_done, AT0 + NS * NB)
            for k in range(0, 4):
                z_back(k)
            last_norm(0)
            z_here(0)
            for k in range(4, 8):
                z_back(k)
            last_norm(1)
            z_here(1)
            for k in range(8, NZP):
                z_back(k)
            act.wait_ge(zp_done, NZP - 2)
            b_high(0, 0, True)
            act.wait_ge(zp_done, NZP)
            b_high(0, 1, False)
            last_norm(2)
            z_here(2)
            last_norm(3)
            z_here(3)
            with act.Fori(1, H) as i:
                b_high(i, 0, True)
                u_high(i - 1, q_u[:, bass.ds(i - 1, 1), 0, :].rearrange("p a f -> p (a f)"))
                b_high(i, 1, False)
            b_high(H, 0, False)
            u_high(H - 1, q_u[:, H - 1, 0, :])
            b_high(H, 1, True)
            act.wait_ge(zd_done, J)
            act.wait_ge(st_x1[0], ST0 + 16 * (NB // 2))
            b_high(H + 1, 0, False)
            u_high(H, u_st[:, 0, :])
            b_high(H + 1, 1, True)
            with act.Fori(H + 2, NB) as i:
                b_high(i, 0, False)
                u_staged(i - 1)
                b_high(i, 1, True)
            u_staged(NB - 1)
            act.wait_ge(st_u, 16 * H)
            with act.Fori(0, NB // 2 - 1) as g:
                for i in range(2):
                    normalise(NB + 2 * g + i, i, ST0 + 16 * (NB // 2) + 16 * g)
            normalise(2 * NB - 2, 0, ST0 + 16 * (NB - 1))

        @block.vector
        def _(dve):
            def step(s, n, ins):
                ins.then_inc(s, 1)
                dve.wait_ge(s, n)

            for c in range(FC):
                dve.wait_ge(ld_w[c], 16)
                nc.vector.bn_stats(wbn[:, c, :], wr[:, c, :]).then_inc(w_stat, 1)
            dve.wait_ge(w_stat, FC)
            nc.vector.bn_aggr(wst[:, 0:2], wbn[:, :, :].rearrange("p c s -> p (c s)")).then_inc(w_mom, 1)
            dve.wait_ge(par_all, 1)
            step(par_step, 1, nc.vector.reciprocal(pinv[:, :], parb[:, :]))
            dve.wait_ge(w_tot, 1)
            step(w_step, 1, nc.vector.tensor_scalar(wst[:, 3:4], wst[:, 3:4], -1.0 / P, None, ALU.mult))
            step(w_step, 2, nc.vector.tensor_scalar(wst[:, 2:3], wst[:, 0:1], wst[:, 3:4], None, ALU.add))
            nc.vector.scalar_tensor_tensor(out=wst[:, 2:3], in0=wst[:, 2:3], scalar=wst[:, 2:3],
                                           in1=wst[:, 1:2], op0=ALU.mult, op1=ALU.add).then_inc(w_step, 1)

            def clip_x(b, blocks):
                for g, (first, _) in enumerate(LOADS):
                    if first == b:
                        dve.wait_ge(ld_x[g], 16)
                v = xr[:, b:b + blocks, :]
                nc.vector.tensor_scalar(v, v, pinv[:, ALPHA_A:ALPHA_A + 1], 1.0, ALU.mult,
                                        ALU.min).then_inc(x_clip, blocks)

            clip_x(0, 1)
            dve.wait_ge(w_tot, 2)
            nc.vector.tensor_scalar(wst[:, 5:6], wst[:, 4:5], WN / (WN - 1.0) / P, None, ALU.mult).then_inc(w_step, 1)
            clip_x(1, 1)
            nc.vector.tensor_scalar(c1[:, :], parb[:, ALPHA_A:ALPHA_A + 1], 1.0 / BITS_A,
                                    parb[:, ALPHA_W:ALPHA_W + 1], ALU.mult, ALU.mult).then_inc(par_step, 1)
            nc.vector.tensor_scalar(k2[:, :], parb[:, ALPHA_A2:ALPHA_A2 + 1], 1.0 / BITS_A,
                                    parb[:, SF:SF + 1], ALU.mult, ALU.mult).then_inc(par_step, 1)
            dve.wait_ge(par_step, 3)
            nc.vector.tensor_scalar(c1[:, :], c1[:, :], pinv[:, ALPHA_A2:ALPHA_A2 + 1], BITS_A / BITS_W,
                                    ALU.mult, ALU.mult).then_inc(par_step, 1)
            nc.vector.tensor_scalar(k2[:, :], k2[:, :], pinv[:, SF:SF + 1], None, ALU.mult).then_inc(par_step, 1)

            def x_lo(b, i):
                dve.wait_ge(xh_done, b + 1)
                nc.vector.scalar_tensor_tensor(out=xit[:, i, 1, :], in0=ps[:, XT + i, :], scalar=-MAGIC,
                                               in1=xit[:, i, 0, :].bitcast(F32), op0=ALU.add,
                                               op1=ALU.subtract).then_inc(xl_done, 1)

            dve.wait_ge(w_tot, 3)
            step(w_step, 5, nc.vector.tensor_scalar(wst[:, 7:8], wst[:, 6:7], pinv[:, ALPHA_W:ALPHA_W + 1], BITS_W,
                                                    ALU.mult, ALU.mult))

            def scale_w(c):
                dve.wait_ge(w_mean, c + 1)
                nc.vector.tensor_scalar(wr[:, c, :], wr[:, c, :], wst[:, 7:8], BITS_W, ALU.mult,
                                        ALU.min).then_inc(w_top, 1)

            def level_w(c):
                dve.wait_ge(w_top, c + 1)
                nc.vector.tensor_scalar(wr[:, c, :], wr[:, c, :], -BITS_W, MAGIC, ALU.max, ALU.add).then_inc(w_level, 1)

            scale_w(0)
            scale_w(1)
            level_w(0)
            level_w(1)
            scale_w(2)
            x_lo(0, 0)
            scale_w(3)
            level_w(2)
            level_w(3)
            clip_x(2, 1)
            x_lo(1, 1)
            clip_x(3, 1)

            def row_max(S, j):
                dve.wait_ge(ld_nat[j], 16 * S + 16)
                nc.vector.tensor_reduce(rmax[:, 2 * j:2 * j + 2],
                                        nat[:, j, :].rearrange("p (h n) -> p h n", h=2), AX.X, ALU.max,
                                        apply_absolute_value=True).then_inc(rmax_done, 1)

            def largest(S):
                dve.wait_ge(rmax_done, J * S + J)
                nc.vector.tensor_reduce(rmx[:, 0:1], rmax[:, :], AX.X, ALU.max).then_inc(rmx_part, 1)

            def scales(S):
                def col(t):
                    return t[:, bass.ds(S, 1)]
                dve.wait_ge(rmx_all, S + 1)
                step(sc_step, 2 * S + 1, nc.vector.tensor_scalar(
                    col(pow2).bitcast(I32), rmx[:, 1:2].bitcast(I32), EXPONENT, None, ALU.bitwise_and))
                step(sc_step, 2 * S + 2, nc.vector.tensor_scalar(
                    col(inv_a), col(pow2), 2.0 ** -100, 1.0 / TOP, ALU.max, ALU.mult))
                nc.vector.reciprocal(col(s_a), col(inv_a))
                nc.vector.tensor_scalar(col(c2), col(inv_a), k2[:, 0:1], None, ALU.mult)
                nc.vector.tensor_scalar(col(c4), col(inv_a), 1.0 / US, None, ALU.mult).then_inc(sc_done, 1)

            def clip(b, i):
                dve.wait_ge(out_free, b + 1)
                nc.vector.tensor_scalar(t1[:, i, :], t1[:, i, :], BITS_A, MAGIC, ALU.min, ALU.add).then_inc(clip_done, 1)

            clip_x(4, 2)

            def pair(g, rows):
                for i in range(2):
                    x_lo(2 * g + i, i)
                    clip(2 * g + i - 2, i)
                    if rows:
                        n = N // 2
                        r = 2 * (g - G0) + i
                        ins = nc.vector.tensor_reduce(rmax[:, r:r + 1], nat[:, g - G0, i * n:(i + 1) * n], AX.X,
                                                      ALU.max, apply_absolute_value=True)
                        if i == 1:
                            ins.then_inc(rmax_done, 1)

            clip_x(6, 2)
            pair(1, False)
            clip_x(8, 2)
            clip_x(10, 2)
            pair(2, False)
            clip_x(12, 2)
            clip_x(14, 2)
            for g in range(G0, G0 + J):
                dve.wait_ge(ld_nat[g - G0], 16)
                pair(g, True)
            largest(0)
            for g in range(G0 + J, NB // 2):
                pair(g, False)
            scales(0)
            clip(NB - 2, 0)

            def at_low(S, k):
                dve.wait_ge(ah_done, S * NB + k + 1)
                nc.vector.scalar_tensor_tensor(out=at_lo[:, k, bass.ts(S, J * P)], in0=ps[:, TB + k % 4, :],
                                               scalar=s_a[:, bass.ds(S, 1)], in1=at_hi[:, k, bass.ts(S, J * P)],
                                               op0=ALU.mult, op1=ALU.subtract).then_inc(at_done, 1)

            def residual(m, n, i, scale):
                dve.wait_ge(out_ready, n + 1)
                dve.wait_ge(ld_xe[i], 16 * (m // 2) + 16)
                dve.wait_ge(ln_out, LN0 + m - 1)
                nc.vector.scalar_tensor_tensor(out=ts[:, i, :], in0=ps[:, OUT + i, :], scalar=scale,
                                               in1=xe[:, i, :], op0=ALU.mult, op1=ALU.add).then_inc(out_free, 1)

            def statistics(m, n, i):
                dve.wait_ge(out_free, n + 1)
                nc.vector.bn_stats(bst[:, 0:6], ts[:, i, :]).then_inc(bs_done, 1)

            def mean_var(m, i):
                dve.wait_ge(consts, 3)
                dve.wait_ge(bs_done, m + 1)
                nc.vector.bn_aggr(mv[:, i, :], bst[:, 0:6]).then_inc(mv_done, 1)

            def moments(m, n, i, scale):
                residual(m, n, i, scale)
                statistics(m, n, i)
                mean_var(m, i)

            def add_high(i, h):
                dve.wait_ge(ld_sa[h], 16 * i + 16)
                nc.vector.scalar_tensor_tensor(out=sa[:, h, :, :], in0=at_hi[:, H * h:H * h + H, bass.ts(i, P)],
                                               scalar=inv_a[:, bass.ds(i // J, 1)], in1=sa[:, h, :, :],
                                               op0=ALU.mult, op1=ALU.add).then_inc(add1, 1)

            def add_low(i, h, diagonal):
                n = 2 * i + h
                dve.wait_ge(add1, n + 1)
                nc.vector.scalar_tensor_tensor(out=sa[:, h, :, :], in0=at_lo[:, H * h:H * h + H, bass.ts(i, P)],
                                               scalar=inv_a[:, bass.ds(i // J, 1)], in1=sa[:, h, :, :],
                                               op0=ALU.mult, op1=ALU.add).then_inc(add2, 1)
                if diagonal:
                    dve.wait_ge(add2, n + 1)
                    d = sa[:, h, bass.ds(i - H * h, 1), :].rearrange("p a c -> p (a c)")
                    nc.vector.scalar_tensor_tensor(out=d, in0=ident[:, :], scalar=2.0, in1=d, op0=ALU.mult,
                                                   op1=ALU.add).then_inc(diag, 1)

            def split_block(S, k, first):
                at_low(S, k)
                m, n, i = S * J - 1, N2 + S * J - 1, (J - 1) % 2
                if k == 3 and not first:
                    residual(m, n, i, c2[:, bass.ds(S - 1, 1)])
                if k == 6 and not first:
                    statistics(m, n, i)
                if k == 7 and not first:
                    mean_var(m, i)

            def superblock(S, first):
                for k in range(NB):
                    split_block(S, k, first)
                    if k == LEAD - 1 and first:
                        clip(NB - 1, 1)
                at = 0
                for j, rows in ((0, 1), (1, 2), (2, 1)):
                    moments(S * J + j, N2 + S * J + j, j % 2, c2[:, bass.ds(S, 1)])
                    if first and j == 0:
                        add_high(0, 0)
                        add_low(0, 0, True)
                    for jj in range(at, at + rows):
                        row_max(S + 1, jj)
                    at += rows
                largest(S + 1)
                scales(S + 1)

            superblock(0, True)
            with dve.Fori(1, NS - 1) as S:
                superblock(S, False)

            def degree_term(S, others):
                if S > 0:
                    dve.wait_ge(dg_step, 4 + S)
                nc.vector.scalar_tensor_tensor(out=deg[:, :], in0=colsum[:, :, S], scalar=inv_a[:, S:S + 1],
                                               in1=others, op0=ALU.mult, op1=ALU.add).then_inc(dg_step, 1)

            for k in range(NB):
                split_block(NS - 1, k, False)
                if k == 9:
                    nc.vector.tensor_reduce(bsc[:, 0:1], pow2[:, :], AX.X, ALU.max).then_inc(dg_step, 1)
                elif k == 10:
                    dve.wait_ge(dg_step, 1)
                    nc.vector.tensor_scalar(bsc[:, 0:1], bsc[:, 0:1], 4.0, 2.0, ALU.mult, ALU.add).then_inc(dg_step, 1)
                elif k == 11:
                    dve.wait_ge(dg_step, 2)
                    nc.vector.tensor_scalar(bsc[:, 3:4].bitcast(I32), bsc[:, 0:1].bitcast(I32), EXPONENT, None,
                                            ALU.bitwise_and).then_inc(dg_step, 1)
                elif k == 12:
                    dve.wait_ge(dg_step, 3)
                    nc.vector.tensor_scalar(bsc[:, 1:2], bsc[:, 3:4], 1.0 / TOP, None, ALU.mult).then_inc(dg_step, 1)
                elif k == 13:
                    dve.wait_ge(dg_step, 4)
                    nc.vector.reciprocal(bsc[:, 2:3], bsc[:, 1:2])
                    dve.wait_ge(rs_done, RS0 + NB)
                    degree_term(0, rowsum[:, :])
                elif k > 13:
                    degree_term(k - 13, deg[:, :])
            degree_term(NS - 1, deg[:, :])
            dve.wait_ge(dg_step, NS + 4)
            step(dg_step, NS + 5, nc.vector.tensor_scalar(deg[:, :], deg[:, :], 0.5, 1.0, ALU.mult, ALU.add))
            nc.vector.tensor_scalar(degm[:, :], deg[:, :], 1e-30, None, ALU.max).then_inc(dg_step, 1)

            def z_back(k):
                dve.wait_ge(zph, k + 1)
                nc.vector.scalar_tensor_tensor(out=z[:, k, 1, :], in0=xz[:, k % 4, :], scalar=dz[:, k:k + 1],
                                               in1=z[:, k, 0, :], op0=ALU.mult, op1=ALU.subtract).then_inc(zp_done, 1)

            def z_here(j):
                k = NZP + j
                dve.wait_ge(zdh, j + 1)
                nc.vector.scalar_tensor_tensor(out=z[:, k, 1, :], in0=x1t[:, j % 2, :], scalar=dz[:, k:k + 1],
                                               in1=z[:, k, 0, :], op0=ALU.mult, op1=ALU.subtract).then_inc(zd_done, 1)

            def b_low(i, h):
                dve.wait_ge(bh_done, 2 * i + h + 1)
                nc.vector.scalar_tensor_tensor(out=bb[:, h, 1, :, :], in0=sa[:, h, :, :], scalar=bsc[:, 2:3],
                                               in1=bb[:, h, 0, :, :], op0=ALU.mult,
                                               op1=ALU.subtract).then_inc(b_done, 1)

            def u_low(i, hi, lo):
                dve.wait_ge(uh_done, i + 1)
                nc.vector.scalar_tensor_tensor(out=lo, in0=bank(i), scalar=eu[:, bass.ds(i, 1)], in1=hi,
                                               op0=ALU.mult, op1=ALU.subtract).then_inc(out_free, 1)

            def last_residual(j):
                residual(NZP + j, N2 + NZP + j, j % 2, c2[:, NS - 1:NS])

            def last_moments(j):
                moments(NZP + j, N2 + NZP + j, j % 2, c2[:, NS - 1:NS])

            last_moments(0)
            add_high(0, 1)
            dve.wait_ge(dg_pow, 1)
            step(dg_step, 11, nc.vector.scalar_tensor_tensor(out=dinv[:, :], in0=deg[:, :], scalar=0.0,
                                                             in1=dpow[:, :], op0=ALU.is_gt, op1=ALU.mult))
            nc.vector.tensor_scalar(eu[:, :], dinv[:, :], bsc[:, 1:2], 0.5 * US / ZS, ALU.mult, ALU.mult)
            step(dg_done, 1, nc.vector.tensor_scalar(dz[:, :], dinv[:, :], ZS, None, ALU.mult))

            for k in range(0, 4):
                z_back(k)
            last_moments(1)
            for k in range(4, 8):
                z_back(k)
            add_low(0, 1, False)
            z_back(8)
            z_back(9)
            last_residual(2)
            statistics(NZP + 2, N2 + NZP + 2, 0)
            b_low(0, 0)
            mean_var(NZP + 2, 0)
            z_back(10)
            z_back(11)
            z_here(0)
            last_residual(3)
            z_here(1)
            statistics(NZP + 3, N2 + NZP + 3, 1)
            b_low(0, 1)
            mean_var(NZP + 3, 1)
            add_high(1, 0)
            z_here(2)
            add_low(1, 0, True)
            z_here(3)

            def rest_of_strip(i, first, hi, lo):
                add_high(i, 1)
                b_low(i, 0)
                add_low(i, 1, not first)
                u_low(i - 1, hi, lo)
                b_low(i, 1)

            def strip(i, first, hi, lo):
                add_high(i, 0)
                add_low(i, 0, first)
                rest_of_strip(i, first, hi, lo)

            def u_block(i, t):
                return q_u[:, bass.ds(i, 1), t, :].rearrange("p a f -> p (a f)")

            rest_of_strip(1, True, q_u[:, 0, 0, :], q_u[:, 0, 1, :])
            with dve.Fori(2, H) as i:
                strip(i, True, u_block(i - 1, 0), u_block(i - 1, 1))
            strip(H, False, q_u[:, H - 1, 0, :], q_u[:, H - 1, 1, :])
            with dve.Fori(H + 1, NB) as i:
                strip(i, False, u_st[:, 0, :], u_st[:, 1, :])
            u_low(NB - 1, u_st[:, 0, :], u_st[:, 1, :])
            with dve.Fori(0, NS - 1) as S:
                for j in range(J):
                    moments(NB + S * J + j, N4 + S * J + j, j % 2, c4[:, bass.ds(S, 1)])
            for j in range(J - 1):
                moments(2 * NB - J + j, N4 + NB - J + j, j % 2, c4[:, NS - 1:NS])
            dve.wait_ge(ld_xe[1], 16 * NB)
            dve.wait_ge(ln_out, LN0 + 2 * NB - 2)
            for h in range(2):
                c = slice(h * F // 2, (h + 1) * F // 2)
                dve.wait_ge(half_ready, h + 1)
                nc.vector.scalar_tensor_tensor(out=ts[:, 1, c], in0=ps[:, TB + h, c], scalar=c4[:, NS - 1:NS],
                                               in1=xe[:, 1, c], op0=ALU.mult, op1=ALU.add).then_inc(half_sum, 1)
                dve.wait_ge(half_sum, h + 1)
                nc.vector.bn_stats(bst[:, 6 * h:6 * h + 6], ts[:, 1, c]).then_inc(bs_done, 1)
            dve.wait_ge(bs_done, 2 * NB + 1)
            nc.vector.bn_aggr(mv[:, 1, :], bst[:, :]).then_inc(mv_done, 1)
            dve.wait_ge(last_rstd, 1)
            dve.wait_ge(st_x1[1], ST0 + 16 * (NB - 1))
            nc.vector.tensor_scalar(x1t[:, 1, :], ts[:, 1, :], mv[:, 1, 0:1], rv[:, 1, 1:2], ALU.subtract,
                                    ALU.mult).then_inc(last_out, 1)

        @block.tensor
        def _(pe):
            pe.wait_ge(ident_done, 1)

            def keep_warm(n):
                for _ in range(n):
                    nc.tensor.transpose(ps[:, TB, 0:P], ident[:, :], ident[:, :])

            keep_warm(WARM)

            def turn_x(b):
                pe.wait_ge(x_int, b + 1)
                if b >= 2:
                    pe.wait_ge(xl_done, b - 1)
                for c in range(FC):
                    mm = nc.tensor.transpose(ps[:, XT + b % 2, c * P:(c + 1) * P], xr[:, b, c * P:(c + 1) * P],
                                             ident[:, :])
                mm.then_inc(xt_done, 1)

            def times_w(b):
                pe.wait_ge(xl_done, b + 1)
                if b >= 2:
                    pe.wait_ge(out_free, b - 1)
                for c in range(FC):
                    if b == 0:
                        pe.wait_ge(wi_done, c + 1)
                    if c == FC // 2 and 0 < b < NB - 2:
                        turn_x(b + 2)
                    for t in range(2):
                        mm = nc.tensor.matmul(ps[:, OUT + b % 2, :], xit[:, b % 2, t, c * P:(c + 1) * P],
                                              wi[:, c, :], start=(c + t == 0), stop=(c == FC - 1 and t == 1))
                mm.then_inc(out_ready, 1)

            def turn_adj(S, k):
                pe.wait_ge(at_done, S * NB + k + 1)
                for j in range(J):
                    if k == 0:
                        pe.wait_ge(ld_nat[j], 16 * S + 16)
                    mm = nc.tensor.transpose(ps[:, TB + k % 4, j * P:(j + 1) * P], nat[:, j, k * P:(k + 1) * P],
                                             ident[:, :])
                mm.then_inc(tb_ready, 1)

            turn_x(0)
            keep_warm(WARM // 10)
            turn_x(1)
            keep_warm(WARM // 5)
            for b in range(NB):
                if b == NB - 1:
                    for k in range(LEAD):
                        turn_adj(0, k)
                times_w(b)
                if b == 0:
                    turn_x(2)

            def superblock(S, last):
                for j in range(J):
                    pe.wait_ge(out_free, N2 + S * J + j - 1)
                    for k in range(NB):
                        if j == 0:
                            if k + LEAD < NB:
                                turn_adj(S, k + LEAD)
                            pe.wait_ge(at_done, AT0 + S * NB + k + 1)
                            pe.wait_ge(q_done, k + 1)
                        if j == J - 1 and k == NB - 4 and not last:
                            for kk in range(LEAD):
                                turn_adj(S + 1, kk)
                        for a in (at_hi, at_lo):
                            mm = nc.tensor.matmul(ps[:, OUT + j % 2, :], a[:, k, bass.ts(S * J + j, P)],
                                                  q_sb[:, k, :], start=(k == 0 and a is at_hi),
                                                  stop=(k == NB - 1 and a is at_lo))
                    mm.then_inc(out_ready, 1)

            with pe.Fori(0, NS - 1) as S:
                superblock(S, False)
            superblock(NS - 1, True)

            def times_z(i, parity, first):
                pe.wait_ge(out_free, N3 + i - 1)
                for h in range(2):
                    pe.wait_ge(b_done, 2 * i + h + 1)
                    for kk in range(H):
                        k = h * H + kk
                        if first and k >= NZP:
                            pe.wait_ge(zd_done, k - NZP + 1)
                        for a, t in ((0, 0), (0, 1), (1, 0)):
                            mm = nc.tensor.matmul(ps[:, OUT + parity, :], bb[:, h, a, kk, :], z[:, k, t, :],
                                                  start=(k == 0 and a + t == 0), stop=(k == NB - 1 and a == 1))
                    mm.then_inc(half_used if h == 0 else out_ready, 1)

            times_z(0, 0, True)
            times_z(1, 1, False)
            with pe.Fori(1, NB // 2) as g:
                times_z(2 * g, 0, False)
                times_z(2 * g + 1, 1, False)

            def times_u(g, first, blocks):
                for i in range(blocks):
                    pe.wait_ge(out_free, N4 + 2 * g + i - 1)
                    for k in range(NB):
                        if first and i == 0:
                            if k < H:
                                pe.wait_ge(out_free, N3 + k + 1)
                            else:
                                pe.wait_ge(ld_u[k - H], 16)
                        u = q_u[:, k, :, :] if k < H else z[:, k, :, :]
                        for a, t in ((at_hi, 0), (at_hi, 1), (at_lo, 0)):
                            mm = nc.tensor.matmul(ps[:, OUT + i, :], a[:, k, bass.ts(2 * g + i, P)], u[:, t, :],
                                                  start=(k == 0 and a is at_hi and t == 0),
                                                  stop=(k == NB - 1 and a is at_lo))
                    mm.then_inc(out_ready, 1)

            times_u(0, True, 2)
            with pe.Fori(1, NB // 2 - 1) as g:
                times_u(g, False, 2)
            times_u(NB // 2 - 1, False, 1)
            for h in range(2):
                c = slice(h * F // 2, (h + 1) * F // 2)
                for k in range(NB):
                    u = q_u[:, k, :, c] if k < H else z[:, k, :, c]
                    for a, t in ((at_hi, 0), (at_hi, 1), (at_lo, 0)):
                        mm = nc.tensor.matmul(ps[:, TB + h, c], a[:, k, N - P:N], u[:, t, :],
                                              start=(k == 0 and a is at_hi and t == 0),
                                              stop=(k == NB - 1 and a is at_lo))
                mm.then_inc(half_ready, 1)


_INS = ["x", "adj", "L0_gnn_adj_scaling_factor", "L0_gnn_weight", "L0_gnn_wgt_alpha", "L0_gnn_act_alpha",
        "L0_gnn_act_alpha2"]


def kernel(**inputs):
    import numpy as _np
    import concourse.bacc as _bacc
    from concourse import mybir as _mybir
    from concourse.bass_utils import run_bass_kernel_spmd as _run

    nc = _bacc.Bacc("TRN2", target_bir_lowering=False, num_devices=1)
    arrays, args = {}, []
    for name in _INS:
        a = _np.ascontiguousarray(inputs[name])
        arrays[f"in_{name}_dram"] = a
        args.append(nc.dram_tensor(f"in_{name}_dram", a.shape, _mybir.dt.from_np(a.dtype), kind="ExternalInput").ap())
    args.append(nc.dram_tensor("out_0_dram", inputs["x"].shape, _mybir.dt.float32, kind="ExternalOutput").ap())
    build(nc, *args)
    r = _run(nc, [arrays], core_ids=[0])
    return r.results[0]["out_0_dram"]
```
